# Optimizing a Trainium2 kernel written in Bass

```python
import numpy as np
import jax
import jax.numpy as jnp

def _softmax(x, axis=-1):
    return jax.nn.softmax(x, axis=axis)

def _gelu(x):
    return jax.nn.gelu(x, approximate=True)

def _silu(x):
    return jax.nn.silu(x)

def _sigmoid(x):
    return jax.nn.sigmoid(x)

def _layernorm(x, axis=-1, eps=1e-05):
    m = jnp.mean(x, axis=axis, keepdims=True)
    v = jnp.var(x, axis=axis, keepdims=True)
    return (x - m) / jnp.sqrt(v + eps)

def _scatter_add(tgt, idx, src, axis=0):
    return tgt.at[idx].add(src)

def _segment_sum(src, seg, n):
    return jax.ops.segment_sum(src, seg, n)
kernel_name = 'mk_xattn_seq_d2_seqx_r8_ff0b7d'

def setup_inputs(seed: int=0):
    np.random.seed(seed)
    _w = jnp.asarray

    def _rec_inputs():
        import jax
        import jax.numpy as jnp
        _rk = jax.random.key(seed)
        x = -0.0002928 + 1 * jax.random.normal(jax.random.fold_in(_rk, 1), (16, 256, 128), jnp.float32)
        _lenS = 256 - jax.random.randint(jax.random.fold_in(_rk, 7), (16,), 0, max(1, 256 // 4) + 1, jnp.int32)
        _lenS2 = 64 - jax.random.randint(jax.random.fold_in(_rk, 8), (16,), 0, max(1, 64 // 4) + 1, jnp.int32)
        _ctx_1024P = jax.random.normal(jax.random.fold_in(_rk, 11), (16, 16, 128), jnp.float32)
        _ctx_1024c = jax.random.dirichlet(jax.random.fold_in(_rk, 511), 0.3 * jnp.ones((16,), jnp.float32), (16, 64))
        _ctx_1024t = jnp.einsum('bsk,bkd->bsd', _ctx_1024c, _ctx_1024P)
        _ctx_1024t = _ctx_1024t * jax.lax.rsqrt(jnp.mean(jnp.square(_ctx_1024t)) + 1e-12) * 0.953939
        ctx_1024 = -1.39393e-06 + 0.999914 * (_ctx_1024t + 0.3 * jax.random.normal(jax.random.fold_in(_rk, 611), (16, 64, 128), jnp.float32))
        _validS = jnp.arange(256)[None, :] < _lenS[:, None]
        _validS2 = jnp.arange(64)[None, :] < _lenS2[:, None]
        _causal = jnp.tril(jnp.ones((256, 256), dtype=bool))
        mask_BxS2_bf1 = jnp.ones((16, 64), dtype=bool)
        return (x, ctx_1024, mask_BxS2_bf1)
    x, ctx_1024, mask_BxS2_bf1 = _rec_inputs()

    def _L0_xattn_setup():
        import math
        import jax, jax.numpy as jnp
        import numpy as np
        D_MODEL = 128
        N_HEADS = 16
        HEAD_DIM = D_MODEL // N_HEADS
        FEATURE_DIM = 16
        WINDOW = 64
        EPS_NORM = 1e-06
        EPS_DEN = 1e-06
        _TRIU_I, _TRIU_J = np.triu_indices(FEATURE_DIM)

        def taylor_feature_map(x):
            B, T, H, d = x.shape
            ones = jnp.ones((B, T, H, 1), dtype=x.dtype)
            outer = jnp.einsum('bthd,bthe->bthde', x, x)
            scale = jnp.full((d, d), 1.0 / math.sqrt(2), dtype=x.dtype)
            scale = scale.at[jnp.arange(d), jnp.arange(d)].set(0.5)
            outer = outer * scale
            quadratic = outer[..., _TRIU_I, _TRIU_J]
            return jnp.concatenate([ones, x, quadratic], axis=-1)

        def rmsnorm(x, w):
            var = jnp.mean(x * x, axis=-1, keepdims=True)
            return x * jax.lax.rsqrt(var + EPS_NORM) * w

        def _forward(x, encoder_out, norm_w, Wq, Wkv, Wqf, Wkf, Wwin, Wout):
            residual = x
            xn = rmsnorm(x, norm_w)
            B, T_dec, _ = xn.shape
            T_enc = encoder_out.shape[1]
            H, hd = (N_HEADS, HEAD_DIM)
            q = (xn @ Wq).reshape(B, T_dec, H, hd)
            kv = (encoder_out @ Wkv).reshape(B, T_enc, 2, H, hd)
            k, v = (kv[:, :, 0], kv[:, :, 1])
            q_phi = taylor_feature_map(q @ Wqf)
            k_phi = taylor_feature_map(k @ Wkf)
            kv_state = jnp.einsum('bshf,bshd->bhfd', k_phi, v)
            k_state = k_phi.sum(axis=1)
            linear_out = jnp.einsum('bthf,bhfd->bthd', q_phi, kv_state)
            normalizer = jnp.einsum('bthf,bhf->bth', q_phi, k_state)[..., None]
            linear_out = (linear_out / (normalizer + EPS_DEN)).reshape(B, T_dec, D_MODEL)
            kv_win = (xn @ Wwin).reshape(B, T_dec, 2, H, hd)
            k_win, v_win = (kv_win[:, :, 0], kv_win[:, :, 1])
            scores = jnp.einsum('bthd,bshd->bhts', q, k_win) * (1.0 / math.sqrt(hd))
            i = jnp.arange(T_dec)[:, None]
            j = jnp.arange(T_dec)[None, :]
            allowed = (j <= i) & (j >= i - WINDOW)
            scores = jnp.where(allowed, scores, jnp.finfo(scores.dtype).min)
            probs = jax.nn.softmax(scores, axis=-1)
            window_out = jnp.einsum('bhts,bshd->bthd', probs, v_win).reshape(B, T_dec, D_MODEL)
            combined = jnp.concatenate([linear_out, window_out], axis=-1)
            return residual + combined @ Wout
        key = jax.random.key(seed)
        ks = jax.random.split(key, 9)
        B, T = (2, 256)
        std = 0.02
        return {'x': jax.random.normal(ks[0], (B, T, D_MODEL), jnp.float32), 'encoder_out': jax.random.normal(ks[1], (B, T, D_MODEL), jnp.float32), 'norm_w': jnp.ones((D_MODEL,), jnp.float32), 'Wq': jax.random.normal(ks[2], (D_MODEL, D_MODEL), jnp.float32) * std, 'Wkv': jax.random.normal(ks[3], (D_MODEL, 2 * D_MODEL), jnp.float32) * std, 'Wqf': jax.random.normal(ks[4], (HEAD_DIM, FEATURE_DIM), jnp.float32) * std, 'Wkf': jax.random.normal(ks[5], (HEAD_DIM, FEATURE_DIM), jnp.float32) * std, 'Wwin': jax.random.normal(ks[6], (D_MODEL, 2 * D_MODEL), jnp.float32) * std, 'Wout': jax.random.normal(ks[7], (2 * D_MODEL, D_MODEL), jnp.float32) * std}
    _L0_xattn_all = _L0_xattn_setup()
    _L0_xattn_in = {k: v for k, v in _L0_xattn_all.items() if k in ('norm_w', 'Wq', 'Wkv', 'Wqf', 'Wkf', 'Wwin', 'Wout')}
    del _L0_xattn_all

    def _L1_xattn_setup():
        import jax, jax.numpy as jnp
        import numpy as np
        NUM_HEADS = 16
        HEAD_DIM = 64
        D_MODEL = 128
        ROPE_BASE = 10000.0

        def rope(x):
            B, S, H, D = x.shape
            inv_freq = 1.0 / ROPE_BASE ** (jnp.arange(0, D, 2, dtype=jnp.float32) / D)
            t = jnp.arange(S, dtype=jnp.float32)
            freqs = jnp.einsum('s,d->sd', t, inv_freq)
            cos = jnp.cos(freqs)[None, :, None, :]
            sin = jnp.sin(freqs)[None, :, None, :]
            x1, x2 = (x[..., 0::2], x[..., 1::2])
            r1 = x1 * cos - x2 * sin
            r2 = x2 * cos + x1 * sin
            out = jnp.stack([r1, r2], axis=-1).reshape(B, S, H, D)
            return out.astype(x.dtype)
        key = jax.random.key(seed)
        ks = jax.random.split(key, 8)
        B, Sq, Skv = (4, 128, 256)
        d = D_MODEL
        hd = NUM_HEADS * HEAD_DIM
        scale = 1.0 / np.sqrt(d)
        return {'decoder_query': jax.random.normal(ks[0], (B, Sq, d), jnp.float32), 'encoder_key_value': jax.random.normal(ks[1], (B, Skv, d), jnp.float32), 'mask': jnp.ones((B, Skv), dtype=bool), 'Wq': jax.random.normal(ks[2], (d, hd), jnp.float32) * scale, 'Wk': jax.random.normal(ks[3], (d, hd), jnp.float32) * scale, 'Wv': jax.random.normal(ks[4], (d, hd), jnp.float32) * scale, 'Wo': jax.random.normal(ks[5], (hd, d), jnp.float32) * (1.0 / np.sqrt(hd)), 'ln_gamma': jnp.ones((d,), jnp.float32), 'ln_beta': jnp.zeros((d,), jnp.float32)}
    _L1_xattn_all = _L1_xattn_setup()
    _L1_xattn_in = {k: v for k, v in _L1_xattn_all.items() if k in ('Wq', 'Wk', 'Wv', 'Wo', 'ln_gamma', 'ln_beta')}
    del _L1_xattn_all
    return {'x': x, 'ctx_1024': ctx_1024, 'mask_BxS2_bf1': mask_BxS2_bf1, 'L0_xattn_norm_w': _L0_xattn_in['norm_w'], 'L0_xattn_Wq': _L0_xattn_in['Wq'], 'L0_xattn_Wkv': _L0_xattn_in['Wkv'], 'L0_xattn_Wqf': _L0_xattn_in['Wqf'], 'L0_xattn_Wkf': _L0_xattn_in['Wkf'], 'L0_xattn_Wwin': _L0_xattn_in['Wwin'], 'L0_xattn_Wout': _L0_xattn_in['Wout'], 'L1_xattn_Wq': _L1_xattn_in['Wq'], 'L1_xattn_Wk': _L1_xattn_in['Wk'], 'L1_xattn_Wv': _L1_xattn_in['Wv'], 'L1_xattn_Wo': _L1_xattn_in['Wo'], 'L1_xattn_ln_gamma': _L1_xattn_in['ln_gamma'], 'L1_xattn_ln_beta': _L1_xattn_in['ln_beta']}

def reference(x, ctx_1024, mask_BxS2_bf1, L0_xattn_norm_w, L0_xattn_Wq, L0_xattn_Wkv, L0_xattn_Wqf, L0_xattn_Wkf, L0_xattn_Wwin, L0_xattn_Wout, L1_xattn_Wq, L1_xattn_Wk, L1_xattn_Wv, L1_xattn_Wo, L1_xattn_ln_gamma, L1_xattn_ln_beta):
    import jax
    import jax.numpy as jnp

    def _L0_xattn_ref(x, encoder_out, norm_w, Wq, Wkv, Wqf, Wkf, Wwin, Wout):
        import math
        import jax, jax.numpy as jnp
        import numpy as np
        D_MODEL = 128
        N_HEADS = 16
        HEAD_DIM = D_MODEL // N_HEADS
        FEATURE_DIM = 16
        WINDOW = 64
        EPS_NORM = 1e-06
        EPS_DEN = 1e-06
        _TRIU_I, _TRIU_J = np.triu_indices(FEATURE_DIM)

        def taylor_feature_map(x):
            B, T, H, d = x.shape
            ones = jnp.ones((B, T, H, 1), dtype=x.dtype)
            outer = jnp.einsum('bthd,bthe->bthde', x, x)
            scale = jnp.full((d, d), 1.0 / math.sqrt(2), dtype=x.dtype)
            scale = scale.at[jnp.arange(d), jnp.arange(d)].set(0.5)
            outer = outer * scale
            quadratic = outer[..., _TRIU_I, _TRIU_J]
            return jnp.concatenate([ones, x, quadratic], axis=-1)

        def rmsnorm(x, w):
            var = jnp.mean(x * x, axis=-1, keepdims=True)
            return x * jax.lax.rsqrt(var + EPS_NORM) * w

        def _forward(x, encoder_out, norm_w, Wq, Wkv, Wqf, Wkf, Wwin, Wout):
            residual = x
            xn = rmsnorm(x, norm_w)
            B, T_dec, _ = xn.shape
            T_enc = encoder_out.shape[1]
            H, hd = (N_HEADS, HEAD_DIM)
            q = (xn @ Wq).reshape(B, T_dec, H, hd)
            kv = (encoder_out @ Wkv).reshape(B, T_enc, 2, H, hd)
            k, v = (kv[:, :, 0], kv[:, :, 1])
            q_phi = taylor_feature_map(q @ Wqf)
            k_phi = taylor_feature_map(k @ Wkf)
            kv_state = jnp.einsum('bshf,bshd->bhfd', k_phi, v)
            k_state = k_phi.sum(axis=1)
            linear_out = jnp.einsum('bthf,bhfd->bthd', q_phi, kv_state)
            normalizer = jnp.einsum('bthf,bhf->bth', q_phi, k_state)[..., None]
            linear_out = (linear_out / (normalizer + EPS_DEN)).reshape(B, T_dec, D_MODEL)
            kv_win = (xn @ Wwin).reshape(B, T_dec, 2, H, hd)
            k_win, v_win = (kv_win[:, :, 0], kv_win[:, :, 1])
            scores = jnp.einsum('bthd,bshd->bhts', q, k_win) * (1.0 / math.sqrt(hd))
            i = jnp.arange(T_dec)[:, None]
            j = jnp.arange(T_dec)[None, :]
            allowed = (j <= i) & (j >= i - WINDOW)
            scores = jnp.where(allowed, scores, jnp.finfo(scores.dtype).min)
            probs = jax.nn.softmax(scores, axis=-1)
            window_out = jnp.einsum('bhts,bshd->bthd', probs, v_win).reshape(B, T_dec, D_MODEL)
            combined = jnp.concatenate([linear_out, window_out], axis=-1)
            return residual + combined @ Wout
        return _forward(x, encoder_out, norm_w, Wq, Wkv, Wqf, Wkf, Wwin, Wout)

    def _L1_xattn_ref(decoder_query, encoder_key_value, mask, Wq, Wk, Wv, Wo, ln_gamma, ln_beta):
        import jax, jax.numpy as jnp
        import numpy as np
        NUM_HEADS = 16
        HEAD_DIM = 64
        D_MODEL = 128
        ROPE_BASE = 10000.0

        def rope(x):
            B, S, H, D = x.shape
            inv_freq = 1.0 / ROPE_BASE ** (jnp.arange(0, D, 2, dtype=jnp.float32) / D)
            t = jnp.arange(S, dtype=jnp.float32)
            freqs = jnp.einsum('s,d->sd', t, inv_freq)
            cos = jnp.cos(freqs)[None, :, None, :]
            sin = jnp.sin(freqs)[None, :, None, :]
            x1, x2 = (x[..., 0::2], x[..., 1::2])
            r1 = x1 * cos - x2 * sin
            r2 = x2 * cos + x1 * sin
            out = jnp.stack([r1, r2], axis=-1).reshape(B, S, H, D)
            return out.astype(x.dtype)
        B, Sq, d = decoder_query.shape
        Skv = encoder_key_value.shape[1]
        H, Dh = (NUM_HEADS, HEAD_DIM)
        q = (decoder_query @ Wq).reshape(B, Sq, H, Dh)
        k = (encoder_key_value @ Wk).reshape(B, Skv, H, Dh)
        v = (encoder_key_value @ Wv).reshape(B, Skv, H, Dh)
        q = rope(q)
        k = rope(k)
        q = q.transpose(0, 2, 1, 3) * (1.0 / jnp.sqrt(jnp.asarray(Dh, q.dtype)))
        k = k.transpose(0, 2, 1, 3)
        v = v.transpose(0, 2, 1, 3)
        scores = jnp.einsum('bhqd,bhkd->bhqk', q, k)
        m = mask[:, None, None, :]
        scores = jnp.where(m, scores, jnp.asarray(-1000000000.0, scores.dtype))
        attn = jax.nn.softmax(scores, axis=-1)
        out = jnp.einsum('bhqk,bhkd->bqhd', attn, v).reshape(B, Sq, H * Dh)
        out = out @ Wo
        x = decoder_query + out
        mu = jnp.mean(x, axis=-1, keepdims=True)
        var = jnp.var(x, axis=-1, keepdims=True)
        y = (x - mu) * jax.lax.rsqrt(var + 0.001) * ln_gamma + ln_beta
        return y
    x = _L0_xattn_ref(x, ctx_1024, L0_xattn_norm_w, L0_xattn_Wq, L0_xattn_Wkv, L0_xattn_Wqf, L0_xattn_Wkf, L0_xattn_Wwin, L0_xattn_Wout)
    x = _L1_xattn_ref(x, ctx_1024, mask_BxS2_bf1, L1_xattn_Wq, L1_xattn_Wk, L1_xattn_Wv, L1_xattn_Wo, L1_xattn_ln_gamma, L1_xattn_ln_beta)
    return x

_drawn_inputs = setup_inputs


def setup_inputs(seed=0):
    import zlib

    import numpy as np

    out = dict(_drawn_inputs(seed))
    spreads = {'L0_xattn_norm_w': (1.0, 0.6),
     'L1_xattn_ln_gamma': (1.0, 0.2),
     'L1_xattn_ln_beta': (0.0, 0.1)}
    factors = {'L0_xattn_Wq': 8.0, 'L0_xattn_Wqf': 8.0, 'L0_xattn_Wkf': 8.0, 'L0_xattn_Wwin': 6.803}
    for name, (base, spread) in spreads.items():
        noise = np.random.default_rng([zlib.crc32(name.encode()), seed]).standard_normal(out[name].shape)
        drawn = base * np.exp(spread * noise) if base else spread * noise
        out[name] = jnp.asarray(drawn.astype(out[name].dtype))
    for name, factor in factors.items():
        out[name] = (out[name] * factor).astype(out[name].dtype)
    return out
```

```python
import concourse.bass as bass
from concourse import mybir
from contextlib import ExitStack
import numpy as np

F32 = mybir.dt.float32
BF16 = mybir.dt.bfloat16
U8 = mybir.dt.uint8
ALU = mybir.AluOpType
ACT = mybir.ActivationFunctionType
AX = mybir.AxisListType

NB, T, D = 16, 256, 128
S = 64
H0, HD0, FD = 16, 8, 16
H1, HD1 = 16, 64
W = 64
PAIRS = 8
NJ = T // 128
SLOTS = 6
KR = SLOTS * HD0
SH = 112
Q_PARTS = (0, 0, 1, 1, 0, 2)
K_PARTS = (0, 1, 0, 1, 2, 0)
BIG = 8e9
NVO = 18


class Batch:

    def __init__(self, half, parity):
        self.h, self.p = half, parity

    def at(self, per, k):
        return self.h * (2 * per) + (self.p * per + k)

    def tile(self, per, j, k):
        return self.at(NJ * per, j * per + k)

    def same(self, per, k):
        return self.h * per + k

    def before(self, per):
        return (self.h + self.p) * per

    @property
    def index(self):
        return self.h * 2 + self.p


def step_order():
    fill = {
        0: {1: ["A.xT"], 2: ["A.qk", "A.hi", "A.rest"], 3: ["A.vw", "A.mid", "A.enc", "A.lo"],
            4: ["A.mem", "K.k0", "K.k1", "A.emid", "A.elo"]},
        1: {1: ["K.kT"], 2: ["K.vo0"], 3: ["K.vo1"], 4: []},
    }
    out = [("A.norm", 0)]
    for j in range(NJ):
        f = {n: [(x, j) for x in v] for n, v in fill[j].items()}
        out += [("B.s0", j), ("B.s1", j), ("C.q0", j), ("B.s2", j), ("C.q1", j), ("B.s3", j), ("B.parts", j)]
        out += f[1] + [("B.shT", j), ("C.t0", j), ("C.t1", j), ("B.lin0", j), ("B.lin1", j)]
        out += f[2] + [("C.s0", j), ("C.s1", j), ("C.parts", j), ("B.st0", j), ("B.st1", j), ("C.shT", j)]
        out += [("B.pv0", j), ("B.st2", j), ("B.pv1", j), ("C.a0", j), ("C.a1", j), ("B.st3", j), ("B.pv2", j)]
        out += [("B.lpv", j), ("B.pv3", j), ("B.norm", j)] + f[3]
        out += [("C.p0", j), ("B.cT", j), ("C.p1", j), ("B.op", j), ("C.y", j), ("B.xT", j)] + f[4] + [("C.fin", j)]
    return out


ORDER = step_order()
NRING = 4
RING = [x for x in ORDER if x[0] in (
    "A.xT", "A.qk", "A.vw", "A.enc", "K.k0", "K.k1", "K.kT", "K.vo0", "K.vo1", "B.s0", "B.s1", "B.s2", "B.s3",
    "B.shT", "B.lin0", "B.lin1", "B.st0", "B.st1", "B.st2", "B.st3", "B.cT", "B.op", "B.xT")]


def stage_of(step, name):
    return {"A": step.a, "B": step.b, "K": step.b, "C": step.c}[name[0]]


class Step:

    def __init__(self, a, b, c, filled, last=None):
        self.a, self.b, self.c, self.filled, self.last = a, b, c, filled, last

    def ring(self, name, j):
        n = RING.index((name, j))
        bank = n % NRING
        mine = sum(1 for m in range(bank, n + 1, NRING) if stage_of(self, RING[m][0]) is not None)
        return bank, self.filled[bank] + mine

    def fills(self):
        out = [0] * NRING
        for m, (name, _) in enumerate(RING):
            if stage_of(self, name) is not None:
                out[m % NRING] += 1
        return out


PEELED = 4


def run_steps(eng, emit):
    filled, step = [0] * NRING, None
    for s in range(PEELED):
        a, b, c = (Batch((s - n) // 2, s % 2 ^ n % 2) if s >= n else None for n in range(3))
        step = Step(a, b, c, filled, step)
        emit(step)
        filled = [x + y for x, y in zip(filled, step.fills())]
    full = Step(1, 1, 1, filled).fills()
    pairs, h = (NB - PEELED) // 2, PEELED // 2
    with eng.Fori(0, pairs) as i:
        for p in range(2):
            base = [i * (2 * n) + (x + p * n) for n, x in zip(full, filled)]
            before = Step(1, 1, 1, [i * (2 * n) + (x + (p - 1) * n) for n, x in zip(full, filled)])
            emit(Step(Batch(i + h, p), Batch(i + (h - 1 + p), 1 - p), Batch(i + (h - 1), p), base, before))
    filled = [x + 2 * pairs * n for x, n in zip(filled, full)]
    last = NB // 2 - 1
    before = Step(1, 1, 1, [x - n for n, x in zip(full, filled)])
    step = Step(None, Batch(last, 1), Batch(last, 0), filled, before)
    emit(step)
    filled = [x + y for x, y in zip(filled, step.fills())]
    emit(Step(None, None, Batch(last, 1), filled, step))


def drained(eng, sems, step, name, j):
    bank, fill = step.ring(name, j)
    wait(eng, sems[bank], fill)


def wait(eng, sem, value):
    if not isinstance(value, int) or value > 0:
        eng.wait_ge(sem, value)


def build(nc, x, ctx, mask, norm_w, wq, wkv, wqf, wkf, wwin, wout, w1q, w1k, w1v, w1o, gamma, beta,
          tab_ident, tab_window, tab_heads, tab_blocks, tab_rope, tab_big, mask_t, out, scratch):
    es = ExitStack()
    with es:
        def sb(name, shape, dt=F32):
            return es.enter_context(nc.sbuf_tensor(name, shape, dt))

        def pb(name, shape):
            return es.enter_context(nc.psum_tensor(name, shape, F32))

        def sem(name):
            return es.enter_context(nc.semaphore(name))

        def two(name, shape, dt=F32):
            return [sb(f"{name}{p}", shape, dt) for p in range(2)]

        wq_s, wkv_s, wwin_s = sb("wq_s", [D, D]), sb("wkv_s", [D, 2 * D]), sb("wwin_s", [D, 2 * D])
        wout_s = sb("wout_s", [D, 2, D])
        nw_s = sb("nw_s", [D, 1])
        qfT, kfT = sb("qfT", [FD, H0, HD0]), sb("kfT", [FD, H0, HD0])
        w1q_s, w1k_s, w1v_s = sb("w1q_s", [D, H1 * HD1]), sb("w1k_s", [D, H1 * HD1]), sb("w1v_s", [D, H1 * HD1])
        w1o_s = sb("w1o_s", [128, PAIRS, D])
        gamma_s, beta_s = sb("gamma_s", [128, D]), sb("beta_s", [128, D])
        ident = sb("ident", [128, 128])
        ident4 = sb("ident4", [128, 4, 128], BF16)
        window_f = sb("window_f", [128, NJ, 128])
        window = sb("window", [128, NJ, 4, 128], BF16)
        heads_f = sb("heads_f", [3 * H1, H1 * S])
        heads = sb("heads", [3 * H1, H1 * S], BF16)
        blocks = sb("blocks", [128, 128])
        cosq, sinq = sb("cosq", [128, NJ, HD1]), sb("sinq", [128, NJ, HD1])
        big3 = sb("big3", [3, 1])
        ones3 = sb("ones3", [3, 128], BF16)
        minus_half = sb("minus_half", [128, 2])
        ones_col = sb("ones_col", [128, 1])
        bd = sb("bd", [128, 128])
        wkT = sb("wkT", [128, 128])
        wkf_s = sb("wkf_s", [D, D])
        wvT = sb("wvT", [128, PAIRS, D])
        wvo = sb("wvo", [D, 2, PAIRS, D])

        xa, ca = two("xa", [128, NJ, D]), two("ca", [S, D])
        xr = two("xr", [128, NJ, D])
        mcol, mrow_u = two("mcol", [S, 1], U8), two("mrow_u", [3, S], U8)
        junk = sb("junk", [128, D])
        ssq, ms, rstd0 = sb("ssq", [128, NJ]), sb("ms", [128, NJ]), sb("rstd0", [128, NJ])
        xs = sb("xs", [128, NJ, D])
        xnT = two("xnT", [D, W + T])
        ctxT = two("ctxT", [D, 2, S])
        hi, mid, lo = sb("hi", [128, 2 * T], BF16), sb("mid", [128, 2 * T], BF16), sb("lo", [128, 2 * T], BF16)
        rest = sb("rest", [128, 2 * T])
        ehi, emid, elo = sb("ehi", [128, S], BF16), sb("emid", [128, S], BF16), sb("elo", [128, S], BF16)
        erest = sb("erest", [128, S])
        qst = two("qst", [128, H0, NJ, 2, W], BF16)
        kst = two("kst", [128, H0, T], BF16)
        est = two("est", [128, H0, S], BF16)
        vw = two("vw", [128, NJ, H0, 2, HD0 + 1])
        vbd = two("vbd", [128, PAIRS, NVO])

        nmx = sb("nmx", [128, H0])
        nrest, nrest2 = sb("nrest", [128, H0]), sb("nrest2", [128, H0])
        shp = sb("shp", [128, 8, H0], BF16)
        shs = sb("shs", [3 * H0, 128], BF16)
        wt = sb("wt", [128, PAIRS, 128])
        pt = sb("pt", [128, H0, 128])
        den, rden = sb("den", [128, 2, H0]), sb("rden", [128, 2, H0])
        comb = sb("comb", [128, 2, D])
        combT = sb("combT", [128, 2, 128])
        x1, x1T = two("x1", [128, NJ, D]), two("x1T", [128, NJ, D])
        coskm = sb("coskm", [S, HD1])
        sinkm = sb("sinkm", [S, HD1])
        ka, kb, kr = sb("ka", [S, 2, 512]), sb("kb", [S, 2, 512]), sb("kr", [S, 2, 512])
        kbd = two("kbd", [128, PAIRS, 128])
        vo = two("vo", [128, PAIRS, D])
        mrow = two("mrow", [3, S], BF16)

        qa, qb, qr = sb("qa", [128, 2, 512]), sb("qb", [128, 2, 512]), sb("qr", [128, 2, 512])
        qT = sb("qT", [128, 2, 4, 128])
        nmx1, nr1, nr2 = sb("nmx1", [128, H1]), sb("nr1", [128, H1]), sb("nr2", [128, H1])
        shp1 = sb("shp1", [128, 8, H1], BF16)
        shs1 = sb("shs1", [3 * H1, 128], BF16)
        pex, pn = sb("pex", [128, 2, 512]), sb("pn", [128, 2, 512])
        lsum, rsum = sb("lsum", [128, H1]), sb("rsum", [128, H1])
        pT = sb("pT", [128, 2, 4, 128])
        z, zn, zg, yo = sb("z", [128, D]), sb("zn", [128, D]), sb("zg", [128, D]), sb("yo", [128, D])
        stats, mv = sb("stats", [128, 6]), sb("mv", [128, 2])
        veps, rstd1 = sb("veps", [128, 1]), sb("rstd1", [128, 1])

        ring = pb("ring", [128, NRING, 512])
        po = pb("po", [128, 512])
        pc = pb("pc", [128, 2, 512])
        pm = pb("pm", [128, 512])

        loaded_w, cleared, consts = sem("loaded_w"), sem("cleared"), sem("consts")
        prep_pe, prep_ev = sem("prep_pe"), sem("prep_ev")
        ring_filled = [sem(f"ring_filled{i}") for i in range(NRING)]
        ring_drained = [sem(f"ring_drained{i}") for i in range(NRING)]
        in_a = [sem(f"in_a{p}") for p in range(2)]
        in_r = [sem(f"in_r{p}") for p in range(2)]
        a_ssq, a_ms, a_rstd, a_xs = sem("a_ssq"), sem("a_ms"), sem("a_rstd"), sem("a_xs")
        a_xnT = sem("a_xnT")
        a_hi, a_mid, a_lo = sem("a_hi"), sem("a_mid"), sem("a_lo")
        a_ehi, a_erest, a_emid, a_elo = sem("a_ehi"), sem("a_erest"), sem("a_emid"), sem("a_elo")
        a_out = [sem(f"a_out{p}") for p in range(2)]
        a_st = [sem(f"a_st{p}") for p in range(2)]
        a_mrow, k_cos = sem("a_mrow"), sem("k_cos")
        k_kr = sem("k_kr")
        b_parts = sem("b_parts")
        b_shift = sem("b_shift")
        b_pv = sem("b_pv")
        b_den, b_comb = sem("b_den"), sem("b_comb")
        c_q, c_rope, c_qr = sem("c_q"), sem("tab_rope"), sem("c_qr")
        c_t, c_qT = sem("c_t"), sem("c_qT")
        c_s, c_nmx, c_parts = sem("c_s"), sem("c_nmx"), sem("c_parts")
        c_shT, c_shs = sem("c_shT"), sem("c_shs")
        c_a, c_exp, c_sum, c_rsum, c_pn = sem("c_a"), sem("c_exp"), sem("c_sum"), sem("c_rsum"), sem("c_pn")
        c_p, c_pT = sem("c_p"), sem("c_pT")
        c_y, c_z, c_stats, c_var, c_veps, c_rstd = (sem(n) for n in ("c_y", "c_z", "c_stats", "c_var", "c_veps", "c_rstd"))
        c_zn, c_zg, c_yo, c_out = sem("c_zn"), sem("c_zg"), sem("c_yo"), sem("c_out")

        block = es.enter_context(nc.Block())
        n_w = [0]

        @block.sync
        def _(sp):
            def load(dst, src):
                sp.dma_start(dst, src).then_inc(loaded_w, 16)
                n_w[0] += 16

            load(qfT[:, 0, :], wqf)
            load(kfT[:, 0, :], wkf)
            load(wq_s[:, :], wq)
            load(wkv_s[:, :], wkv)
            load(wwin_s[:, :], wwin)
            load(wout_s[:, :, :], wout.rearrange("(k p) n -> p k n", p=128))
            load(nw_s[:, :], norm_w.rearrange("(p a) -> p a", a=1))
            load(ident[:, :], tab_ident)
            load(window_f[:, :, :], tab_window)
            load(heads_f[:, :], tab_heads)
            load(blocks[:, :], tab_blocks)
            load(cosq[:, :, :], tab_rope[0].rearrange("(j t) d -> t j d", t=128))
            load(sinq[:, :, :], tab_rope[1].rearrange("(j t) d -> t j d", t=128))
            load(big3[:, :], tab_big)
            load(w1v_s[:, :], w1v)
            load(w1o_s[:, :, :], w1o.rearrange("(k p) n -> p k n", p=128))
            load(w1k_s[:, :], w1k)
            load(w1q_s[:, :], w1q)
            load(gamma_s[:, :], gamma.rearrange("(a n) -> a n", a=1).broadcast_to([128, D]))
            load(beta_s[:, :], beta.rearrange("(a n) -> a n", a=1).broadcast_to([128, D]))

            def emit(st):
                for name, j in ORDER:
                    b = stage_of(st, name)
                    if b is None:
                        continue
                    p = b.p
                    if name == "A.norm":
                        wait(sp, a_xs, b.at(2, 2) - 4)
                        wait(sp, a_xnT, b.at(1, 1) - 2)
                        wait(sp, k_cos, b.at(2, 2) - 4)
                        wait(sp, a_mrow, b.at(1, 1) - 2)
                        rows = bass.ds(b.index, 1)
                        sp.dma_start(xa[p][:, :, :], x[rows].rearrange("a (j t) c -> t (a j) c", t=128)).then_inc(in_a[p], 16)
                        sp.dma_start(ca[p][:, :], ctx[rows].rearrange("a s c -> s (a c)")).then_inc(in_a[p], 16)
                        sp.dma_start(mcol[p][:, :], mask_t[:, rows], allow_slow_non_contiguous=True).then_inc(in_a[p], 16)
                        sp.dma_start(mrow_u[p][:, :], mask[rows].broadcast_to([3, S])).then_inc(in_a[p], 16)
                        if st.last is not None and st.last.b is not None:
                            drained(sp, ring_drained, st.last, "B.op", NJ - 1)
                        sp.dma_start(xr[p][:, :, :], x[rows].rearrange("a (j t) c -> t (a j) c", t=128)).then_inc(in_r[p], 16)
                    if name == "A.mem":
                        img = scratch[p]
                        parts = ((a_hi, hi, 0), (a_mid, mid, 1), (a_lo, lo, 2))
                        for ready, tile, part in parts:
                            wait(sp, ready, b.at(1, 1))
                            for i in range(SLOTS):
                                if Q_PARTS[i] == part:
                                    sp.dma_start(img[0][i].rearrange("d h c -> h d c"), tile[:, 0:T]).then_inc(a_out[p], 16)
                                if K_PARTS[i] == part:
                                    sp.dma_start(img[1][i].rearrange("d h c -> h d c"), tile[:, T:2 * T]).then_inc(a_out[p], 16)
                        for ready, tile, part in ((a_ehi, ehi, 0), (a_emid, emid, 1), (a_elo, elo, 2)):
                            wait(sp, ready, b.at(1, 1))
                            for i in range(SLOTS):
                                if K_PARTS[i] == part:
                                    sp.dma_start(img[2][i].rearrange("d h c -> h d c")[:, :, 0:S], tile[:, :]).then_inc(a_out[p], 16)
                        sp.wait_ge(a_out[p], b.same(18 * 16, 18 * 16))
                        qi, ki, ei = (img[n].rearrange("i d h c -> (i d) h c") for n in range(3))
                        for e in range(2):
                            r = slice(64 * e, 64 * e + KR)
                            for k in range(NJ):
                                block_at = W * (NJ * e + k)
                                sp.dma_start(qst[p][r, :, k, e, :], qi[:, :, block_at:block_at + W]).then_inc(a_st[p], 16)
                            if e == 0:
                                sp.dma_start(kst[p][r, :, W:T], ki[:, :, 0:T - W]).then_inc(a_st[p], 16)
                            else:
                                sp.dma_start(kst[p][r, :, :], ki[:, :, :]).then_inc(a_st[p], 16)
                            sp.dma_start(est[p][r, :, :], ei[:, :, 0:S]).then_inc(a_st[p], 16)
                    if name == "B.shT":
                        drained(sp, ring_drained, st, "B.shT", j)
                        for e in range(2):
                            sp.dma_start(qst[p][SH:SH + 3, :, j, e, :], shs[:, W * e:W * e + W]).then_inc(b_shift, 16)
                    if name == "C.fin":
                        sp.wait_ge(c_yo, b.tile(1, j, 1))
                        dst = out[bass.ds(b.index, 1)][:, 128 * j:128 * j + 128, :].rearrange("a t c -> t (a c)")
                        sp.dma_start(dst, yo[:, :]).then_inc(c_out, 16)

            run_steps(sp, emit)
            sp.wait_ge(c_out, 16 * NJ * NB)

        @block.tensor
        def _(pe):
            mm = nc.tensor.matmul
            tr = nc.tensor.transpose

            pe.wait_ge(loaded_w, n_w[0])
            pe.wait_ge(consts, 7)
            mm(ring[:, 0, 0:128], kfT[:, :, :].rearrange("f h d -> f (h d)"), qfT[:, :, :].rearrange("f h d -> f (h d)"),
               start=True, stop=True)
            tr(ring[:, 1, 0:128], wkv_s[:, 0:D], ident[:, :]).then_inc(prep_pe, 1)
            pe.wait_ge(prep_ev, 2)
            mm(ring[:, 0, 0:128], wkT[:, :], bd[:, :], start=True, stop=True).then_inc(prep_pe, 1)
            for i in range(2):
                for k in range(4):
                    last = tr(ring[:, 2 + i, 128 * k:128 * k + 128], w1v_s[:, 128 * (4 * i + k):128 * (4 * i + k) + 128],
                              ident[:, :])
                last.then_inc(prep_pe, 1)
            pe.wait_ge(prep_ev, 5)
            for n in range(4):
                e, i = n // 2, n % 2
                for k in range(4):
                    r = slice(64 * e, 64 * e + 64)
                    last = mm(pc[:, n % 2, 128 * k:128 * k + 128] if n < 2 else ring[:, n, 128 * k:128 * k + 128],
                              wvT[r, 4 * i + k, :], w1o_s[r, 4 * i + k, :], start=True, stop=True)
                last.then_inc(prep_pe, 1)
            pe.wait_ge(prep_ev, 9)
            pe.wait_ge(cleared, 20)

            def emit(st):
                for name, j in ORDER:
                    b = stage_of(st, name)
                    if b is None:
                        continue
                    p = b.p
                    if (name, j) in RING:
                        bank, fill = st.ring(name, j)
                        wait(pe, ring_drained[bank], fill - 1)
                        r = ring[:, bank, :]

                    if name == "A.xT":
                        pe.wait_ge(a_xs, b.at(2, 2))
                        pe.wait_ge(in_a[p], b.same(64, 64))
                        for k in range(NJ):
                            tr(r[:, 128 * k:128 * k + 128], xs[:, k, :], ident[:, :])
                        tr(r[:, 256:256 + S], ca[p][:, :], ident[0:S, 0:S]).then_inc(ring_filled[bank], 1)
                    if name == "A.qk":
                        pe.wait_ge(a_xnT, b.at(1, 1))
                        xq = xnT[p][:, W:W + T].rearrange("c (j e t) -> c e j t", e=2, t=W)
                        mm(r[:, 0:T], wq_s[:, :], xq, start=True, stop=True)
                        mm(r[:, T:2 * T], wwin_s[:, 0:D], xnT[p][:, W:W + T], start=True, stop=True)\
                            .then_inc(ring_filled[bank], 1)
                    if name == "A.vw":
                        for n in range(4):
                            last = mm(r[:, 128 * n:128 * n + 128], xnT[p][:, W * n:W * n + 128], wwin_s[:, D:2 * D],
                                      start=True, stop=True)
                        last.then_inc(ring_filled[bank], 1)
                    if name == "A.enc":
                        drained(pe, ring_drained, st, "A.xT", j)
                        c2 = ctxT[p][:, :, :].rearrange("c a s -> c (a s)")
                        mm(r[:, 0:S], wkf_s[:, :], c2[:, 0:S], start=True, stop=True)
                        mm(r[:, S:S + D], c2, wkv_s[:, D:2 * D], start=True, stop=True).then_inc(ring_filled[bank], 1)

                    if name in ("K.k0", "K.k1"):
                        i = int(name[-1])
                        mm(r[0:S, :], ctxT[p][:, 0, :], w1k_s[:, 512 * i:512 * i + 512], start=True, stop=True)\
                            .then_inc(ring_filled[bank], 1)
                    if name == "K.kT":
                        pe.wait_ge(k_kr, b.at(2, 2))
                        mm(r[:, 0:S], kr[:, 0, 0:128], ident[0:S, 0:S], start=True, stop=True)
                        for k in range(1, PAIRS):
                            last = tr(r[:, S * k:S * k + S], kr[:, k // 4, 128 * (k % 4):128 * (k % 4) + 128], ident[0:S, 0:S])
                        last.then_inc(ring_filled[bank], 1)
                    if name in ("K.vo0", "K.vo1"):
                        i = int(name[-1])
                        for e in range(2):
                            last = mm(r[64 * e:64 * e + 64, :], ctxT[p][:, e, :],
                                      wvo[:, e, 4 * i:4 * i + 4, :].rearrange("c k n -> c (k n)"), start=True, stop=True)
                        last.then_inc(ring_filled[bank], 1)

                    if name in ("B.s0", "B.s1", "B.s2", "B.s3"):
                        g = int(name[-1])
                        if g == 0 and j == 0:
                            pe.wait_ge(a_st[p], b.same(128, 128))
                        mm(r, ident4[:, 0, :], window[:, j, :, :].rearrange("t h r -> t (h r)"), start=True, stop=False)
                        for k in range(4):
                            h = 4 * g + k
                            last = mm(r[:, 128 * k:128 * k + 128], qst[p][0:SH, h, j, :, :].rearrange("r e t -> r (e t)"),
                                      kst[p][0:SH, h, 128 * j:128 * j + 128], start=False, stop=k == 3)
                        last.then_inc(ring_filled[bank], 1)
                    if name == "B.shT":
                        pe.wait_ge(b_parts, b.tile(5, j, 5))
                        tr(r[:, 0:64].bitcast(BF16), shp[:, :, :].rearrange("t k h -> t (k h)"), ident4[:, 0, :])\
                            .then_inc(ring_filled[bank], 1)
                    if name in ("B.lin0", "B.lin1"):
                        i = int(name[-1])
                        for k in range(4):
                            for e in range(2):
                                h = 2 * (4 * i + k) + e
                                last = mm(r[64 * e:64 * e + 64, 128 * k:128 * k + 128], est[p][0:SH, h, :],
                                          qst[p][0:SH, h, j, :, :].rearrange("r e t -> r (e t)"), start=True, stop=True)
                        last.then_inc(ring_filled[bank], 1)
                    if name in ("B.st0", "B.st1", "B.st2", "B.st3"):
                        g = int(name[-1])
                        if g == 0:
                            pe.wait_ge(b_shift, b.tile(32, j, 32))
                        mm(r, window[:, j, 0, :], ident4[:, :, :].rearrange("t h r -> t (h r)"), start=True, stop=False)
                        for k in range(4):
                            h = 4 * g + k
                            last = mm(r[:, 128 * k:128 * k + 128], kst[p][0:SH + 3, h, 128 * j:128 * j + 128],
                                      qst[p][0:SH + 3, h, j, :, :].rearrange("r e t -> r (e t)"), start=False, stop=k == 3)
                        last.then_inc(ring_filled[bank], 1)
                    if name in ("B.pv0", "B.pv1", "B.pv2", "B.pv3"):
                        g = int(name[-1])
                        if g == 0:
                            wait(pe, b_comb, b.tile(3, j, 0))
                            if j == 0:
                                drained(pe, ring_drained, st.last, "A.vw", 0)
                                drained(pe, ring_drained, st.last, "A.enc", 0)
                        drained(pe, ring_drained, st, f"B.st{g}", j)
                        for k in range(4):
                            h = 4 * g + k
                            last = mm(po[:, NVO * h:NVO * h + NVO], pt[:, h, :], vw[p][:, j, h, :, :].rearrange("r e d -> r (e d)"),
                                      start=True, stop=True)
                        last.then_inc(b_pv, 1)
                    if name == "B.lpv":
                        for i in range(2):
                            drained(pe, ring_drained, st, f"B.lin{i}", j)
                        for k in range(PAIRS):
                            c = NVO * (H0 + k)
                            last = mm(po[:, c:c + NVO], wt[:, k, :], vbd[p][:, k, :], start=True, stop=True)
                        last.then_inc(b_pv, 1)
                    if name == "B.cT":
                        pe.wait_ge(b_comb, b.tile(3, j, 3))
                        for k in range(2):
                            last = tr(r[:, 128 * k:128 * k + 128], comb[:, k, :], ident[:, :])
                        last.then_inc(ring_filled[bank], 1)
                    if name == "B.op":
                        drained(pe, ring_drained, st, "B.cT", j)
                        for k in range(2):
                            last = mm(r[:, 0:128], combT[:, k, :], wout_s[:, k, :], start=k == 0, stop=k == 1)
                        last.then_inc(ring_filled[bank], 1)
                    if name == "B.xT":
                        drained(pe, ring_drained, st, "B.op", j)
                        tr(r[:, 0:128], x1[p][:, j, :], ident[:, :]).then_inc(ring_filled[bank], 1)

                    if name in ("C.q0", "C.q1"):
                        i = int(name[-1])
                        drained(pe, ring_drained, st.last, "B.xT", j)
                        wait(pe, c_pT, b.tile(2, j, 0))
                        mm(pc[:, i, :], x1T[p][:, j, :], w1q_s[:, 512 * i:512 * i + 512], start=True, stop=True)\
                            .then_inc(c_q, 1)
                    if name in ("C.t0", "C.t1"):
                        i = int(name[-1])
                        pe.wait_ge(c_qr, b.tile(2, j, i + 1))
                        for k in range(4):
                            last = tr(pc[:, i, 128 * k:128 * k + 128], qr[:, i, 128 * k:128 * k + 128], ident[:, :])
                        last.then_inc(c_t, 1)
                    if name in ("C.s0", "C.s1"):
                        i = int(name[-1])
                        if i == 0 and j == 0:
                            drained(pe, ring_drained, st.last, "K.kT", 1)
                            pe.wait_ge(a_mrow, b.at(1, 1))
                        pe.wait_ge(c_qT, b.tile(2, j, i + 1))
                        masked = mrow[p][:, :].rearrange("k (a s) -> k a s", a=1).broadcast_to([3, 8, S])
                        mm(pc[:, i, :], ones3[:, :], masked, start=True, stop=False)
                        for k in range(4):
                            last = mm(pc[:, i, 128 * k:128 * k + 128], qT[:, i, k, :], kbd[p][:, 4 * i + k, :],
                                      start=False, stop=k == 3)
                        last.then_inc(c_s, 1)
                    if name == "C.shT":
                        pe.wait_ge(c_parts, b.tile(5, j, 5))
                        wait(pe, c_z, b.tile(1, j, 0))
                        tr(pm[:, 0:64].bitcast(BF16), shp1[:, :, :].rearrange("t k h -> t (k h)"), ident4[:, 0, :])\
                            .then_inc(c_shT, 1)
                    if name in ("C.a0", "C.a1"):
                        i = int(name[-1])
                        pe.wait_ge(c_shs, b.tile(1, j, 1))
                        mm(pc[:, i, :], shs1[:, :], heads[:, 512 * i:512 * i + 512], start=False, stop=True,
                           skip_group_check=True)\
                            .then_inc(c_a, 1)
                    if name in ("C.p0", "C.p1"):
                        i = int(name[-1])
                        pe.wait_ge(c_pn, b.tile(2, j, i + 1))
                        for k in range(4):
                            last = tr(pc[:, i, 128 * k:128 * k + 128], pn[:, i, 128 * k:128 * k + 128], ident[:, :])
                        last.then_inc(c_p, 1)
                    if name == "C.y":
                        if j == 0:
                            drained(pe, ring_drained, st.last, "K.vo0", 1)
                            drained(pe, ring_drained, st.last, "K.vo1", 1)
                        pe.wait_ge(c_pT, b.tile(2, j, 2))
                        for k in range(PAIRS):
                            last = mm(pm[:, 0:128], pT[:, k // 4, k % 4, :], vo[p][:, k, :], start=k == 0, stop=k == PAIRS - 1)
                        last.then_inc(c_y, 1)

            run_steps(pe, emit)

        @block.scalar
        def _(act):
            cp = nc.scalar.copy
            act.wait_ge(loaded_w, n_w[0])
            act.wait_ge(prep_pe, 1)
            cp(wkT[:, :], ring[:, 1, 0:128]).then_inc(prep_ev, 1)
            act.wait_ge(prep_pe, 2)
            cp(wkf_s[:, :], ring[:, 0, 0:128]).then_inc(prep_ev, 1)
            for i in range(2):
                act.wait_ge(prep_pe, 3 + i)
                cp(wvT[:, 4 * i:4 * i + 4, :].rearrange("p k n -> p (k n)"), ring[:, 2 + i, :]).then_inc(prep_ev, 1)
            for n in range(4):
                e, i = n // 2, n % 2
                act.wait_ge(prep_pe, 5 + n)
                cp(wvo[:, e, 4 * i:4 * i + 4, :].rearrange("p k n -> p (k n)"), pc[:, n, :] if n < 2 else ring[:, n, :])\
                    .then_inc(prep_ev, 1)

            def emit(st):
                for name, j in ORDER:
                    b = stage_of(st, name)
                    if b is None:
                        continue
                    p = b.p
                    if (name, j) in RING:
                        bank, fill = st.ring(name, j)
                        r = ring[:, bank, :]

                    if name == "A.norm":
                        act.wait_ge(in_a[p], b.same(64, 64))
                        wait(act, a_ms, b.at(1, 0))
                        for k in range(NJ):
                            wait(act, a_ssq, b.at(2, k))
                            nc.scalar.activation(junk[:, :], xa[p][:, k, :], ACT.Square, accum_out=ssq[:, k:k + 1])\
                                .then_inc(a_ssq, 1)
                    if name == "A.qk":
                        act.wait_ge(ring_filled[bank], fill)
                        wait(act, a_out[1 - p], b.before(18 * 16))
                        wait(act, b_pv, b.at(5 * NJ, 5 * NJ) - 10 * NJ)
                        cp(hi[:, :], r).then_inc(a_hi, 1)
                    if name == "A.mid":
                        drained(act, ring_drained, st, "A.qk", 0)
                        cp(mid[:, :], rest[:, :]).then_inc(a_mid, 1)
                    if name == "A.vw":
                        act.wait_ge(ring_filled[bank], fill)
                        for k in range(NJ):
                            last = cp(vw[p][:, k, :, :, 0:HD0].rearrange("r h e d -> r e h d"),
                                      r[:, 256 * k:256 * k + 256].rearrange("r (e h d) -> r e h d", e=2, d=HD0))
                        last.then_inc(ring_drained[bank], 1)
                    if name == "A.enc":
                        act.wait_ge(ring_filled[bank], fill)
                        cp(ehi[:, :], r[:, 0:S]).then_inc(a_ehi, 1)
                    if name == "A.emid":
                        act.wait_ge(a_erest, b.at(1, 1))
                        cp(emid[:, :], erest[:, :]).then_inc(a_emid, 1)
                    if name == "K.kT":
                        act.wait_ge(ring_filled[bank], fill)
                        wait(act, c_s, b.at(2 * NJ, 2 * NJ) - 4 * NJ)
                        for e in range(2):
                            q = slice(64 * e, 64 * e + 64)
                            last = cp(kbd[p][q, :, q], r[q, :].rearrange("d (k s) -> d k s", s=S))
                        last.then_inc(ring_drained[bank], 1)
                    if name in ("K.vo0", "K.vo1"):
                        i = int(name[-1])
                        act.wait_ge(ring_filled[bank], fill)
                        wait(act, c_y, b.at(NJ, NJ) - 2 * NJ)
                        last = cp(vo[p][:, 4 * i:4 * i + 4, :].rearrange("s k n -> s (k n)"), r)
                        last.then_inc(ring_drained[bank], 1)

                    if name == "B.shT":
                        act.wait_ge(ring_filled[bank], fill)
                        wait(act, b_shift, b.tile(32, j, 0))
                        last = cp(shs[:, :], r[0:48, 0:64].bitcast(BF16))
                        last.then_inc(ring_drained[bank], 1)
                    if name in ("B.lin0", "B.lin1"):
                        i = int(name[-1])
                        act.wait_ge(ring_filled[bank], fill)
                        wait(act, b_pv, b.tile(5, j, 0))
                        last = nc.scalar.activation(wt[:, 4 * i:4 * i + 4, :].rearrange("s k t -> s (k t)"), r, ACT.Square,
                                                    bias=ones_col[:, :], scale=0.5)
                        last.then_inc(ring_drained[bank], 1)
                    if name in ("B.st0", "B.st1", "B.st2", "B.st3"):
                        g = int(name[-1])
                        act.wait_ge(ring_filled[bank], fill)
                        last = nc.scalar.activation(pt[:, 4 * g:4 * g + 4, :].rearrange("r h t -> r (h t)"), r, ACT.Exp,
                                                    scale=float(HD0) ** -0.5)
                        last.then_inc(ring_drained[bank], 1)
                    if name == "B.cT":
                        act.wait_ge(ring_filled[bank], fill)
                        last = cp(combT[:, :, :].rearrange("c k t -> c (k t)"), r[:, 0:256])
                        last.then_inc(ring_drained[bank], 1)
                    if name == "B.xT":
                        act.wait_ge(ring_filled[bank], fill)
                        wait(act, c_q, b.at(2 * NJ, 2 * NJ) - 4 * NJ)
                        last = cp(x1T[p][:, j, :], r[:, 0:128])
                        last.then_inc(ring_drained[bank], 1)

                    if name in ("C.t0", "C.t1"):
                        i = int(name[-1])
                        act.wait_ge(c_t, b.tile(2, j, i + 1))
                        cp(qT[:, i, :, :].rearrange("d k t -> d (k t)"), pc[:, i, :]).then_inc(c_qT, 1)
                    if name == "C.shT":
                        act.wait_ge(c_shT, b.tile(1, j, 1))
                        cp(shs1[:, :], pm[0:48, 0:64].bitcast(BF16)).then_inc(c_shs, 1)
                    if name in ("C.a0", "C.a1"):
                        i = int(name[-1])
                        act.wait_ge(c_a, b.tile(2, j, i + 1))
                        wait(act, c_pn, b.tile(2, j, 0))
                        nc.scalar.activation(pex[:, i, :], pc[:, i, :], ACT.Exp, scale=HD1 ** -0.5).then_inc(c_exp, 1)
                    if name in ("C.p0", "C.p1"):
                        i = int(name[-1])
                        act.wait_ge(c_p, b.tile(2, j, i + 1))
                        wait(act, c_y, b.tile(1, j, 0))
                        cp(pT[:, i, :, :].rearrange("s k t -> s (k t)"), pc[:, i, :]).then_inc(c_pT, 1)

            act.wait_ge(consts, 8)
            run_steps(act, emit)

        @block.vector
        def _(dve):
            v = nc.vector
            dve.wait_ge(loaded_w, n_w[0])
            for k in range(4):
                last = v.tensor_copy(ident4[:, k, :], ident[:, :])
            last.then_inc(consts, 1)
            for k in range(4):
                last = v.tensor_copy(window[:, :, k, :], window_f[:, :, :])
            last.then_inc(consts, 1)
            v.tensor_copy(heads[:, :], heads_f[:, :]).then_inc(consts, 1)
            v.memset(ones3[:, :], 1.0).then_inc(consts, 1)
            v.memset(minus_half[:, :], -0.5).then_inc(consts, 1)
            v.tensor_copy(qfT[:, 1:H0, :], qfT[:, 0:1, :].broadcast_to([FD, H0 - 1, HD0])).then_inc(consts, 1)
            v.tensor_copy(kfT[:, 1:H0, :], kfT[:, 0:1, :].broadcast_to([FD, H0 - 1, HD0])).then_inc(consts, 1)
            v.memset(ones_col[:, :], 1.0).then_inc(consts, 1)
            v.memset(shp[:, 3:8, :], 0.0)
            v.memset(shp1[:, 3:8, :], 0.0)
            dve.wait_ge(prep_pe, 1)
            v.tensor_tensor(out=bd[:, :], in0=ring[:, 0, 0:128], in1=blocks[:, :], op=ALU.mult).then_inc(prep_ev, 1)

            def rope(dst_a, dst_b, src, cos, sin, n, done):
                heads_n = src.shape[-1] // HD1
                v.tensor_tensor(out=dst_a.rearrange("t (h d) -> t h d", d=HD1), in0=src.rearrange("t (h d) -> t h d", d=HD1),
                                in1=cos.broadcast_to([n, heads_n, HD1]), op=ALU.mult)
                s4 = src.rearrange("t (h i two) -> t h i two", two=2, i=HD1 // 2)
                d4 = dst_b.rearrange("t (h i two) -> t h i two", two=2, i=HD1 // 2)
                c4 = sin.rearrange("t a (i two) -> t a i two", two=2)
                for e in range(2):
                    last = v.tensor_tensor(out=d4[:, :, :, e], in0=s4[:, :, :, 1 - e],
                                           in1=c4[:, :, :, e].broadcast_to([n, heads_n, HD1 // 2]), op=ALU.mult)
                last.then_inc(done, 1)

            def parts(done, base, src, rest1, rest2, dst):
                v.tensor_copy(dst[:, 0, :], src).then_inc(done, 1)
                dve.wait_ge(done, base(1))
                v.tensor_tensor(out=rest1, in0=src, in1=dst[:, 0, :], op=ALU.subtract).then_inc(done, 1)
                dve.wait_ge(done, base(2))
                v.tensor_copy(dst[:, 1, :], rest1).then_inc(done, 1)
                dve.wait_ge(done, base(3))
                v.tensor_tensor(out=rest2, in0=rest1, in1=dst[:, 1, :], op=ALU.subtract).then_inc(done, 1)
                dve.wait_ge(done, base(4))
                v.tensor_copy(dst[:, 2, :], rest2).then_inc(done, 1)

            def emit(st):
                for name, j in ORDER:
                    b = stage_of(st, name)
                    if b is None:
                        continue
                    p = b.p
                    if (name, j) in RING:
                        bank, fill = st.ring(name, j)
                        r = ring[:, bank, :]

                    if name == "A.norm":
                        dve.wait_ge(in_a[p], b.same(64, 64))
                        v.tensor_scalar(mrow[p][:, :], mrow_u[p][:, :], -1.0, big3[:, :], ALU.add, ALU.mult).then_inc(a_mrow, 1)
                        dve.wait_ge(a_ssq, b.at(2, 2))
                        v.tensor_scalar(ms[:, :], ssq[:, :], 1.0 / D, 1e-6, ALU.mult, ALU.add).then_inc(a_ms, 1)
                        dve.wait_ge(a_rstd, b.at(1, 1))
                        for k in range(NJ):
                            v.tensor_scalar(xs[:, k, :], xa[p][:, k, :], rstd0[:, k:k + 1], None, ALU.mult).then_inc(a_xs, 1)
                    if name == "A.xT":
                        dve.wait_ge(ring_filled[bank], fill)
                        v.tensor_scalar(xnT[p][:, W:W + T], r[:, 0:T], nw_s[:, :], None, ALU.mult).then_inc(a_xnT, 1)
                        last = v.tensor_copy(ctxT[p][:, :, :], r[:, T:T + S].rearrange("c (a s) -> c a s", a=1).broadcast_to([D, 2, S]))
                        last.then_inc(ring_drained[bank], 1)
                    if name == "A.rest":
                        bank, fill = st.ring("A.qk", j)
                        dve.wait_ge(a_hi, b.at(1, 1))
                        wait(dve, a_lo, b.at(1, 0))
                        last = v.tensor_tensor(out=rest[:, :], in0=ring[:, bank, :], in1=hi[:, :], op=ALU.subtract)
                        last.then_inc(ring_drained[bank], 1)
                    if name == "A.lo":
                        dve.wait_ge(a_mid, b.at(1, 1))
                        v.tensor_tensor(out=lo[:, :], in0=rest[:, :], in1=mid[:, :], op=ALU.subtract).then_inc(a_lo, 1)
                    if name == "A.enc":
                        dve.wait_ge(a_ehi, b.at(1, 1))
                        wait(dve, a_elo, b.at(1, 0))
                        v.tensor_tensor(out=erest[:, :], in0=r[:, 0:S], in1=ehi[:, :], op=ALU.subtract).then_inc(a_erest, 1)
                        for e in range(2):
                            q = slice(64 * e, 64 * e + 64)
                            src = r[q, S:S + D].rearrange("s (k e d) -> s k e d", e=2, d=HD0)
                            last = v.tensor_copy(vbd[p][q, :, 9 * e:9 * e + HD0], src[:, :, e, :])
                        last.then_inc(ring_drained[bank], 1)
                    if name == "A.elo":
                        dve.wait_ge(a_emid, b.at(1, 1))
                        v.tensor_tensor(out=elo[:, :], in0=erest[:, :], in1=emid[:, :], op=ALU.subtract).then_inc(a_elo, 1)

                    if name in ("K.k0", "K.k1"):
                        i = int(name[-1])
                        if i == 0:
                            v.tensor_scalar(coskm[:, :], cosq[0:S, 0, :], mcol[p][:, :], None, ALU.mult).then_inc(k_cos, 1)
                            v.tensor_scalar(sinkm[:, :], sinq[0:S, 0, :], mcol[p][:, :], None, ALU.mult).then_inc(k_cos, 1)
                            dve.wait_ge(k_cos, b.at(2, 2))
                            wait(dve, k_kr, b.at(2, 0))
                        dve.wait_ge(ring_filled[bank], fill)
                        one = "s (a d) -> s a d"
                        rope(ka[:, i, :], kb[:, i, :], r[0:S, :], coskm[:, :].rearrange(one, a=1),
                             sinkm[:, :].rearrange(one, a=1), S, ring_drained[bank])

                    if name in ("B.s0", "B.s1", "B.s2", "B.s3"):
                        g = int(name[-1])
                        dve.wait_ge(ring_filled[bank], fill)
                        last = v.tensor_reduce(out=nmx[:, 4 * g:4 * g + 4], in_=r.rearrange("t (h r) -> t h r", r=128),
                                               axis=AX.X, op=ALU.max, negate=True)
                        last.then_inc(ring_drained[bank], 1)
                    if name == "B.parts":
                        drained(dve, ring_drained, st, "B.s3", j)
                        parts(b_parts, lambda k: b.tile(5, j, k), nmx[:, :], nrest[:, :], nrest2[:, :], shp)
                    if name == "B.norm":
                        dve.wait_ge(b_pv, b.tile(5, j, 5))
                        lin = po[:, NVO * H0:NVO * (H0 + PAIRS)].rearrange("t (h d) -> t h d", d=HD0 + 1)
                        win = po[:, 0:NVO * H0].rearrange("t (h d) -> t h d", d=NVO)
                        v.tensor_scalar(den[:, 0, :], lin[:, :, HD0], 1e-6, None, ALU.add)
                        for e in range(2):
                            q = slice(64 * e, 64 * e + 64)
                            last = v.tensor_copy(den[q, 1, :], win[q, :, 9 * e + HD0])
                        last.then_inc(b_den, 1)
                        dve.wait_ge(b_den, b.tile(2, j, 1))
                        v.reciprocal(rden[:, :, :], den[:, :, :]).then_inc(b_den, 1)
                        dve.wait_ge(b_den, b.tile(2, j, 2))
                        v.tensor_tensor(out=comb[:, 0, :].rearrange("t (h d) -> t h d", d=HD0), in0=lin[:, :, 0:HD0],
                                        in1=rden[:, 0, :].rearrange("t (h a) -> t h a", a=1).broadcast_to([128, H0, HD0]),
                                        op=ALU.mult).then_inc(b_comb, 1)
                        for e in range(2):
                            q = slice(64 * e, 64 * e + 64)
                            v.tensor_tensor(out=comb[q, 1, :].rearrange("t (h d) -> t h d", d=HD0),
                                            in0=win[q, :, 9 * e:9 * e + HD0],
                                            in1=rden[q, 1, :].rearrange("t (h a) -> t h a", a=1).broadcast_to([64, H0, HD0]),
                                            op=ALU.mult).then_inc(b_comb, 1)
                    if name == "B.op":
                        dve.wait_ge(ring_filled[bank], fill)
                        dve.wait_ge(in_r[p], b.same(16, 16))
                        wait(dve, c_z, b.at(NJ, NJ) - 2 * NJ)
                        last = v.tensor_tensor(out=x1[p][:, j, :], in0=r[:, 0:128], in1=xr[p][:, j, :], op=ALU.add)
                        last.then_inc(ring_drained[bank], 1)

                    if name in ("C.q0", "C.q1"):
                        i = int(name[-1])
                        dve.wait_ge(c_q, b.tile(2, j, i + 1))
                        wait(dve, c_qr, b.tile(2, j, 0))
                        rope(qa[:, i, :], qb[:, i, :], pc[:, i, :], cosq[:, j:j + 1, :], sinq[:, j:j + 1, :], 128, c_rope)
                    if name in ("C.s0", "C.s1"):
                        i = int(name[-1])
                        dve.wait_ge(c_s, b.tile(2, j, i + 1))
                        v.tensor_reduce(out=nmx1[:, 8 * i:8 * i + 8], in_=pc[:, i, :].rearrange("t (h s) -> t h s", s=S),
                                        axis=AX.X, op=ALU.max, negate=True).then_inc(c_nmx, 1)
                    if name == "C.parts":
                        dve.wait_ge(c_nmx, b.tile(2, j, 2))
                        parts(c_parts, lambda k: b.tile(5, j, k), nmx1[:, :], nr1[:, :], nr2[:, :], shp1)
                    if name in ("C.a0", "C.a1"):
                        i = int(name[-1])
                        q = slice(8 * i, 8 * i + 8)
                        dve.wait_ge(c_exp, b.tile(2, j, i + 1))
                        wait(dve, c_pn, b.tile(2, j, 0))
                        v.tensor_reduce(out=lsum[:, q], in_=pex[:, i, :].rearrange("t (h s) -> t h s", s=S), axis=AX.X,
                                        op=ALU.add).then_inc(c_sum, 1)
                        dve.wait_ge(c_sum, b.tile(2, j, i + 1))
                        v.reciprocal(rsum[:, q], lsum[:, q]).then_inc(c_rsum, 1)
                    if name == "C.y":
                        dve.wait_ge(c_y, b.tile(1, j, 1))
                        wait(dve, c_zn, b.tile(1, j, 0))
                        v.tensor_tensor(out=z[:, :], in0=pm[:, 0:128], in1=x1[p][:, j, :], op=ALU.add).then_inc(c_z, 1)
                        dve.wait_ge(c_z, b.tile(1, j, 1))
                        v.bn_stats(stats[:, :], z[:, :]).then_inc(c_stats, 1)
                        dve.wait_ge(loaded_w, n_w[0])
                        dve.wait_ge(c_stats, b.tile(1, j, 1))
                        v.bn_aggr(mv[:, :], stats[:, :]).then_inc(c_var, 1)
                        dve.wait_ge(c_var, b.tile(1, j, 1))
                        v.tensor_scalar(veps[:, :], mv[:, 1:2], 1e-3, None, ALU.add).then_inc(c_veps, 1)
                    if name == "C.fin":
                        dve.wait_ge(c_rstd, b.tile(1, j, 1))
                        wait(dve, c_zg, b.tile(1, j, 0))
                        v.tensor_scalar(zn[:, :], z[:, :], mv[:, 0:1], rstd1[:, :], ALU.subtract, ALU.mult).then_inc(c_zn, 1)

            run_steps(dve, emit)

        @block.gpsimd
        def _(pool):
            g = nc.gpsimd
            n = 0
            for p in range(2):
                for part, value in ((qst[p][:, :, :, :, :], 0.0), (kst[p][0:96, :, :], 0.0), (kst[p][96:128, :, :], 1.0),
                                    (est[p][:, :, :], 0.0), (vw[p][:, :, :, :, :], 1.0), (vbd[p][:, :, :], 0.0),
                                    (vbd[p][0:64, :, HD0:HD0 + 1], 1.0), (vbd[p][64:128, :, NVO - 1:NVO], 1.0),
                                    (kbd[p][:, :, :], 0.0), (xnT[p][:, 0:W], 0.0)):
                    wait(pool, cleared, n)
                    g.memset(part, value).then_inc(cleared, 1)
                    n += 1
            pool.wait_ge(cleared, n)
            pool.wait_ge(loaded_w, n_w[0])
            pool.wait_ge(consts, 5)

            def emit(st):
                for name, j in ORDER:
                    b = stage_of(st, name)
                    if b is None:
                        continue
                    p = b.p
                    if name == "A.norm":
                        pool.wait_ge(a_ms, b.at(1, 1))
                        wait(pool, a_xs, b.at(2, 0))
                        g.tensor_tensor(out=rstd0[:, :], in0=ms[:, :], in1=minus_half[:, :], op=ALU.pow).then_inc(a_rstd, 1)
                    if name in ("K.k0", "K.k1"):
                        i = int(name[-1])
                        drained(pool, ring_drained, st, name, j)
                        g.tensor_tensor(out=kr[:, i, :], in0=ka[:, i, :], in1=kb[:, i, :], op=ALU.add).then_inc(k_kr, 1)
                    if name in ("C.q0", "C.q1"):
                        i = int(name[-1])
                        pool.wait_ge(c_rope, b.tile(2, j, i + 1))
                        wait(pool, c_t, b.tile(2, j, 0))
                        g.tensor_tensor(out=qr[:, i, :], in0=qa[:, i, :], in1=qb[:, i, :], op=ALU.add).then_inc(c_qr, 1)
                    if name in ("C.a0", "C.a1"):
                        i = int(name[-1])
                        pool.wait_ge(c_rsum, b.tile(2, j, i + 1))
                        wait(pool, c_p, b.tile(2, j, 0))
                        rs = rsum[:, 8 * i:8 * i + 8].rearrange("t (h a) -> t h a", a=1).broadcast_to([128, 8, S])
                        g.tensor_tensor(out=pn[:, i, :].rearrange("t (h s) -> t h s", s=S),
                                        in0=pex[:, i, :].rearrange("t (h s) -> t h s", s=S), in1=rs, op=ALU.mult)\
                            .then_inc(c_pn, 1)
                    if name == "C.y":
                        pool.wait_ge(c_veps, b.tile(1, j, 1))
                        g.tensor_tensor(out=rstd1[:, :], in0=veps[:, :], in1=minus_half[:, 0:1], op=ALU.pow).then_inc(c_rstd, 1)
                    if name == "C.fin":
                        pool.wait_ge(c_zn, b.tile(1, j, 1))
                        g.tensor_tensor(out=zg[:, :], in0=zn[:, :], in1=gamma_s[:, :], op=ALU.mult).then_inc(c_zg, 1)
                        pool.wait_ge(c_zg, b.tile(1, j, 1))
                        wait(pool, c_out, b.tile(16, j, 0))
                        g.tensor_tensor(out=yo[:, :], in0=zg[:, :], in1=beta_s[:, :], op=ALU.add).then_inc(c_yo, 1)

            run_steps(pool, emit)


def constants():
    f = np.float32
    t = np.arange(128)
    r = np.arange(128)
    tt, rr = (t % W)[:, None], r[None, :]
    ok = (rr >= tt) & (rr <= tt + W)
    first = ok & ((rr >= W) | (t[:, None] >= W))
    window = np.where(np.stack([first, ok], 1), f(0), f(-1e30)).astype(f)
    row = np.arange(3 * H1) % H1
    col = np.arange(H1 * S) // S
    heads = (row[:, None] == col[None, :]).astype(f)
    blk = np.arange(128) // HD0
    blocks = (blk[:, None] == blk[None, :]).astype(f)
    inv = (f(1.0) / np.power(f(10000.0), np.arange(0, HD1, 2, dtype=f) / f(HD1))).astype(f)
    ang = (np.arange(T, dtype=f)[:, None] * inv[None, :]).astype(f)
    cos, sin = np.cos(ang).astype(f), np.sin(ang).astype(f)
    rope = np.stack([np.repeat(cos, 2, 1), np.stack([-sin, sin], -1).reshape(T, HD1)]).astype(f)
    left, big = f(BIG), []
    for _ in range(3):
        top = (left.view(np.uint32) & np.uint32(0xFFFF0000)).view(f)
        big.append(top)
        left = f(left - top)
    return {"tab_ident": np.eye(128, dtype=f), "tab_window": window, "tab_heads": heads, "tab_blocks": blocks, "tab_rope": rope,
            "tab_big": np.array(big, f).reshape(3, 1)}


_INS = ["x", "ctx_1024", "mask_BxS2_bf1", "L0_xattn_norm_w", "L0_xattn_Wq", "L0_xattn_Wkv", "L0_xattn_Wqf",
        "L0_xattn_Wkf", "L0_xattn_Wwin", "L0_xattn_Wout", "L1_xattn_Wq", "L1_xattn_Wk", "L1_xattn_Wv", "L1_xattn_Wo",
        "L1_xattn_ln_gamma", "L1_xattn_ln_beta"]


def kernel(**inputs):
    import concourse.bacc as bacc
    from concourse.bass_utils import run_bass_kernel_spmd

    nc = bacc.Bacc("TRN2", target_bir_lowering=False, num_devices=1)
    arrays, args = {}, []
    for name in _INS:
        a = np.ascontiguousarray(inputs[name])
        if a.dtype == np.bool_:
            a = a.view(np.uint8)
            mask_t = np.ascontiguousarray(a.T)
        if name in ("L0_xattn_Wqf", "L0_xattn_Wkf"):
            a = np.ascontiguousarray(a.T)
        arrays["in_" + name] = a
        args.append(nc.dram_tensor("in_" + name, a.shape, mybir.dt.from_np(a.dtype), kind="ExternalInput").ap())
    for name, a in constants().items():
        arrays[name] = a
        args.append(nc.dram_tensor(name, a.shape, F32, kind="ExternalInput").ap())
    arrays["mask_t"] = mask_t
    args.append(nc.dram_tensor("mask_t", mask_t.shape, U8, kind="ExternalInput").ap())
    out = nc.dram_tensor("out_0", (NB, T, D), F32, kind="ExternalOutput").ap()
    scratch = [[nc.dram_tensor(f"stack{p}_{n}", (SLOTS, HD0, H0, T), BF16, kind="Internal").ap() for n in range(3)]
               for p in range(2)]
    build(nc, *args, out, scratch)
    r = run_bass_kernel_spmd(nc, [arrays], core_ids=[0])
    return r.results[0]["out_0"]
```

```python
import concourse.bass as bass
from concourse import mybir
from contextlib import ExitStack
import numpy as np

F32 = mybir.dt.float32
BF16 = mybir.dt.bfloat16
U8 = mybir.dt.uint8
ALU = mybir.AluOpType
ACT = mybir.ActivationFunctionType
AX = mybir.AxisListType

NB, T, D = 16, 256, 128
S = 64
H0, HD0, FD = 16, 8, 16
H1, HD1 = 16, 64
W = 64
PAIRS = 8
NJ = T // 128
SLOTS = 6
KR = SLOTS * HD0
KS = 112
Q_PARTS = (0, 0, 1, 1, 0, 2)
K_PARTS = (0, 1, 0, 1, 2, 0)
BIG = 8e9
NVO = 18


class Batch:

    def __init__(self, half, parity, loop=None):
        self.h, self.p, self.loop = half if loop is None else loop + half, parity, loop
        self.offset = half

    def of(self, array):
        pairs = array.rearrange({2: "(h q) s -> q h s", 3: "(h q) s c -> q h s c"}[len(array.shape)], q=2)[self.p]
        return pairs[bass.ds(self.offset, 1)] if self.loop is None else pairs[self.offset:][bass.ds(self.loop, 1)]

    def at(self, per, k):
        return self.h * (2 * per) + (self.p * per + k)

    def tile(self, per, j, k):
        return self.at(NJ * per, j * per + k)

    def same(self, per, k):
        return self.h * per + k

    def before(self, per):
        return (self.h + self.p) * per


ORDER = [(x.split(":")[0], int(x.split(":")[1])) for x in """
    A.xT:0 B.lin0:0 B.s0:0 B.s1:0 B.d0:0 B.d1:0 C.q0:0 B.lin1:0 C.q1:0 B.e0:0 A.enc:0 B.s2:0 B.e1:0 B.t0:0 A.qk:0
    B.d2:0 B.t1:0 B.e2:0 B.s3:0 A.rest:0 B.pv0:0 B.s0:1 B.s1:1 B.pv1:0 C.t0:0 B.d3:0 B.d0:1 C.q0:1 A.mid:0 C.s0:0
    B.d1:1 C.d0:0 B.e3:0 C.t1:0 B.e0:1 B.t2:0 C.q1:1 C.e0:0 B.lpv:0 C.s1:0 P.v0:1 C.n0:0 C.d1:0 C.t0:1 B.t3:0
    B.s2:1 A.w0:0 C.e1:0 B.e1:1 A.emid:0 A.hi:0 C.n1:0 B.d2:1 B.pv2:0 B.pv3:0 C.t1:1 B.norm:0 C.p0:0 P.k0:0 B.t0:1
    B.lin0:1 C.s0:1 A.elo:0 B.lin1:1 C.d0:1 B.s3:1 B.e2:1 B.pv0:1 C.e0:1 C.p1:0 A.load:0 A.lo:0 B.d3:1 B.t1:1
    C.s1:1 A.w1:0 B.lpv:1 C.d1:1 L.load:0 P.v1:1 C.e1:1 P.v2:1 C.n0:1 P.v3:1 C.n1:1 B.pv1:1 L.norm:1 B.cT:0 B.e3:1
    C.y:0 P.k1:0 A.w2:0 C.p0:1 K.vo:1 B.t2:1 C.p1:1 A.rd:0 B.t3:1 B.op:0 B.pv2:1 B.pv3:1 C.fin:0 B.norm:1 C.y:1
    B.cT:1 B.xT:0 K.kT:1 B.op:1 C.fin:1 A.vw:0 B.xT:1
""".split()]
NRING = 7
RING = [x for x in ORDER if x[0] in (
    "A.xT", "A.qk", "A.vw", "A.enc", "P.k0", "P.k1", "P.v0", "P.v1", "P.v2", "P.v3", "K.kT", "B.s0", "B.s1", "B.s2", "B.s3",
    "B.lin0", "B.lin1", "B.t0", "B.t1", "B.t2", "B.t3", "B.cT", "B.op", "B.xT",
    "C.q0", "C.q1", "C.t0", "C.t1", "C.s0", "C.s1", "C.p0", "C.p1", "C.y")]


def stage_of(step, name):
    if name[0] == "P":
        return step.b if step.b is not None and step.b.p == 0 else None
    return {"L": step.l, "A": step.a, "B": step.b, "K": step.b, "C": step.c}[name[0]]


class Step:

    def __init__(self, stages, filled, last=None):
        self.l, self.a, self.b, self.c = stages
        self.filled, self.last = filled, last

    def ring(self, name, j):
        n = RING.index((name, j))
        bank = n % NRING
        mine = sum(1 for m in range(bank, n + 1, NRING) if stage_of(self, RING[m][0]) is not None)
        return bank, self.filled[bank] + mine

    def fills(self):
        out = [0] * NRING
        for m, (name, _) in enumerate(RING):
            if stage_of(self, name) is not None:
                out[m % NRING] += 1
        return out


PEELED = 4


STAGES = 4


def run_steps(eng, emit):
    filled, step = [0] * NRING, None

    def plain(s, step, filled):
        stages = [Batch((s - n) // 2, (s - n) % 2) if 0 <= s - n < NB else None for n in range(STAGES)]
        step = Step(stages, filled, step)
        emit(step)
        return step, [x + y for x, y in zip(filled, step.fills())]

    for s in range(PEELED):
        step, filled = plain(s, step, filled)

    def looped(i, p, filled, last=None, back=0):
        stages = [Batch((PEELED + p - n) // 2 - back, (PEELED + p - n) % 2, i) for n in range(STAGES)]
        return Step(stages, filled, last)

    full = [looped(0, p, filled).fills() for p in range(2)]
    per_pair = [x + y for x, y in zip(*full)]
    pairs = (NB - PEELED) // 2
    with eng.Fori(0, pairs) as i:
        even = [i * n + x for n, x in zip(per_pair, filled)]
        odd = [i * n + (x + m) for n, x, m in zip(per_pair, filled, full[0])]
        before = [i * n + (x - m) for n, x, m in zip(per_pair, filled, full[1])]
        emit(looped(i, 0, even, looped(i, 1, before, back=1)))
        emit(looped(i, 1, odd, looped(i, 0, even)))
    filled = [x + pairs * n for x, n in zip(filled, per_pair)]
    step = looped(pairs - 1, 1, [x - n for n, x in zip(full[1], filled)])
    for s in range(NB, NB + STAGES - 1):
        step, filled = plain(s, step, filled)


def drained(eng, sems, step, name, j, own=None):
    bank, fill = step.ring(name, j)
    if bank != own:
        wait(eng, sems[bank], fill)


def wait(eng, sem, value):
    if not isinstance(value, int) or value > 0:
        eng.wait_ge(sem, value)


def build(nc, x, ctx, mask, norm_w, wq, wkv, wqf, wkf, wwin, wout, w1q, w1k, w1v, w1o, gamma, beta,
          tab_ident, tab_window, tab_blocks, tab_rope, tab_big, out, scratch):
    es = ExitStack()
    with es:
        def sb(name, shape, dt=F32):
            return es.enter_context(nc.sbuf_tensor(name, shape, dt))

        def pb(name, shape):
            return es.enter_context(nc.psum_tensor(name, shape, F32))

        def sem(name):
            return es.enter_context(nc.semaphore(name))

        def two(name, shape, dt=F32):
            return [sb(f"{name}{p}", shape, dt) for p in range(2)]

        wq_s, wkv_s, wwin_s = sb("wq_s", [D, D]), sb("wkv_s", [D, 2 * D]), sb("wwin_s", [D, 2 * D])
        wout_s = sb("wout_s", [D, 2, D])
        nw_s = sb("nw_s", [D, 1])
        qfT, kfT = sb("qfT", [FD, H0, HD0]), sb("kfT", [FD, H0, HD0])
        w1q_s, w1k_s, w1v_s = sb("w1q_s", [D, H1 * HD1]), sb("w1k_s", [D, H1 * HD1]), sb("w1v_s", [D, H1 * HD1])
        w1o_s = sb("w1o_s", [128, PAIRS, D])
        gamma_s, beta_s = sb("gamma_s", [128, D]), sb("beta_s", [128, D])
        ident = sb("ident", [128, 128])
        ident4 = sb("ident4", [128, 4, 128], BF16)
        window_f = sb("window_f", [128, NJ, 128])
        window = sb("window", [128, NJ, 4, 128], BF16)
        blocks = sb("blocks", [128, 128])
        cosq, sinq = sb("cosq", [128, NJ, HD1]), sb("sinq", [128, NJ, HD1])
        big3 = sb("big3", [3, 1])
        ones3 = sb("ones3", [3, 128], BF16)
        minus_half = sb("minus_half", [128, 2])
        ones_col = sb("ones_col", [128, 1])
        bd = sb("bd", [128, 128])
        wkT = sb("wkT", [128, 128])
        wkf_s = sb("wkf_s", [D, D])
        wvT = sb("wvT", [128, PAIRS, D])
        wvo = sb("wvo", [D, 2, PAIRS, D])

        xa, ca = two("xa", [128, NJ, D]), two("ca", [S, D])
        xr = two("xr", [128, NJ, D])
        mcol, mrow_u = sb("mcol", [128, 1], U8), two("mrow_u", [3, S], U8)
        junk = sb("junk", [128, D])
        ssq, ms, rstd0 = sb("ssq", [128, NJ]), sb("ms", [128, NJ]), sb("rstd0", [128, NJ])
        xs = sb("xs", [128, NJ, D])
        xnT = two("xnT", [D, W + T])
        ctxT = two("ctxT", [D, 2, S])
        ctxP = sb("ctxP", [D, 2, S])
        hi, mid, lo = sb("hi", [128, 2 * T], BF16), sb("mid", [128, 2 * T], BF16), sb("lo", [128, 2 * T], BF16)
        rest = sb("rest", [128, 2 * T])
        ehi, emid, elo = sb("ehi", [128, S], BF16), sb("emid", [128, S], BF16), sb("elo", [128, S], BF16)
        erest = sb("erest", [128, S])
        qst = two("qst", [128, H0, NJ, 2, W], BF16)
        kst = two("kst", [128, H0, T], BF16)
        est = two("est", [128, H0, S], BF16)
        vw = two("vw", [128, NJ, H0, 2, HD0 + 1])
        vbd = two("vbd", [128, PAIRS, NVO])

        mx = sb("mx", [128, H0])
        pw = sb("pw", [128, H0, 128])
        wt = sb("wt", [128, PAIRS, 128])
        pt = sb("pt", [128, H0, 128])
        den, rden = sb("den", [128, 2, H0]), sb("rden", [128, 2, H0])
        comb = sb("comb", [128, 2, D])
        combT = sb("combT", [128, 2, 128])
        x1, x1T = two("x1", [128, NJ, D]), two("x1T", [128, NJ, D])
        cosk, sink = sb("cosk", [128, HD1]), sb("sink", [128, HD1])
        coskm, sinkm = sb("coskm", [128, HD1]), sb("sinkm", [128, HD1])
        ka, kb, kr = sb("ka", [128, 2, 512]), sb("kb", [128, 2, 512]), sb("kr", [128, 2, 512])
        vpair = sb("vpair", [128, 2, PAIRS, D])
        kbd = two("kbd", [128, PAIRS, 128])
        vo = two("vo", [128, PAIRS, D])
        mrow = two("mrow", [3, S], BF16)

        qa, qb, qr = sb("qa", [128, 2, 512]), sb("qb", [128, 2, 512]), sb("qr", [128, 2, 512])
        qT = sb("qT", [128, 2, 4, 128])
        mx1 = sb("mx1", [128, H1])
        pex, pn = sb("pex", [128, 2, 512]), sb("pn", [128, 2, 512])
        lsum, rsum = sb("lsum", [128, H1]), sb("rsum", [128, H1])
        pT = sb("pT", [128, 2, 4, 128])
        z, zn, zg, yo = sb("z", [128, D]), sb("zn", [128, D]), sb("zg", [128, D]), sb("yo", [128, NJ, D])
        stats, mv = sb("stats", [128, 6]), sb("mv", [128, 2])
        veps, rstd1 = sb("veps", [128, 1]), sb("rstd1", [128, 1])

        ring = pb("ring", [128, NRING, 512])
        po = pb("po", [128, 512])

        loaded_w, cleared, consts = sem("loaded_w"), sem("cleared"), sem("consts")
        prep_pe, prep_ev = sem("prep_pe"), sem("prep_ev")
        ring_filled = [sem(f"ring_filled{i}") for i in range(NRING)]
        ring_drained = [sem(f"ring_drained{i}") for i in range(NRING)]
        in_a = [sem(f"in_a{p}") for p in range(2)]
        in_m = [sem(f"in_m{p}") for p in range(2)]
        in_r = [sem(f"in_r{p}") for p in range(2)]
        a_ssq, a_ms, a_rstd, a_xs = sem("a_ssq"), sem("a_ms"), sem("a_rstd"), sem("a_xs")
        a_xnT = sem("a_xnT")
        a_hi, a_mid, a_lo = sem("a_hi"), sem("a_mid"), sem("a_lo")
        a_ehi, a_erest, a_emid, a_elo = sem("a_ehi"), sem("a_erest"), sem("a_emid"), sem("a_elo")
        a_out = [sem(f"a_out{p}") for p in range(2)]
        a_st = [sem(f"a_st{p}") for p in range(2)]
        k_mrow, k_cos, k_kr = sem("k_mrow"), sem("k_cos"), sem("k_kr")
        k_vo = [sem(f"k_vo{p}") for p in range(2)]
        b_max, b_exp, b_pv = sem("b_max"), sem("b_exp"), sem("b_pv")
        b_den, b_comb = sem("b_den"), sem("b_comb")
        c_qr = sem("c_qr")
        c_max, c_exp, c_sum, c_rsum, c_pn = sem("c_max"), sem("c_exp"), sem("c_sum"), sem("c_rsum"), sem("c_pn")
        c_z, c_var, c_veps, c_rstd = (sem(n) for n in ("c_z", "c_var", "c_veps", "c_rstd"))
        c_zn, c_zg, c_yo = sem("c_zn"), sem("c_zg"), sem("c_yo")
        c_out = [sem(f"c_out{j}") for j in range(NJ)]

        block = es.enter_context(nc.Block())
        n_w = [0]

        @block.sync
        def _(sp):
            def load(dst, src):
                sp.dma_start(dst, src).then_inc(loaded_w, 16)
                n_w[0] += 16

            load(qfT[:, 0, :], wqf)
            load(kfT[:, 0, :], wkf)
            load(wq_s[:, :], wq)
            load(wkv_s[:, :], wkv)
            load(wwin_s[:, :], wwin)
            load(wout_s[:, :, :], wout.rearrange("(k p) n -> p k n", p=128))
            load(nw_s[:, :], norm_w.rearrange("(p a) -> p a", a=1))
            load(ident[:, :], tab_ident)
            load(window_f[:, :, :], tab_window)
            load(blocks[:, :], tab_blocks)
            load(cosq[:, :, :], tab_rope[0].rearrange("(j t) d -> t j d", t=128))
            load(sinq[:, :, :], tab_rope[1].rearrange("(j t) d -> t j d", t=128))
            for p in range(2):
                load(cosk[S * p:S * p + S, :], tab_rope[0][0:S, :])
                load(sink[S * p:S * p + S, :], tab_rope[1][0:S, :])
            load(big3[:, :], tab_big)
            load(w1v_s[:, :], w1v)
            load(w1o_s[:, :, :], w1o.rearrange("(k p) n -> p k n", p=128))
            load(w1k_s[:, :], w1k)
            load(w1q_s[:, :], w1q)
            load(gamma_s[:, :], gamma.rearrange("(a n) -> a n", a=1).broadcast_to([128, D]))
            load(beta_s[:, :], beta.rearrange("(a n) -> a n", a=1).broadcast_to([128, D]))

            def emit(st):
                for name, j in ORDER:
                    b = stage_of(st, name)
                    if b is None:
                        continue
                    p = b.p
                    if name == "L.load":
                        wait(sp, a_xs, b.at(2, 2) - 4)
                        wait(sp, a_xnT, b.at(1, 1) - 2)
                        sp.dma_start(xa[p][:, :, :], b.of(x).rearrange("a (j t) c -> t (a j) c", t=128)).then_inc(in_a[p], 16)
                        sp.dma_start(ca[p][:, :], b.of(ctx).rearrange("a s c -> s (a c)")).then_inc(in_a[p], 16)
                    if name == "A.load":
                        if st.last is not None and st.last.b is not None:
                            drained(sp, ring_drained, st.last, "B.op", NJ - 1)
                        sp.dma_start(xr[p][:, :, :], b.of(x).rearrange("a (j t) c -> t (a j) c", t=128)).then_inc(in_r[p], 16)
                        sp.dma_start(mcol[S * p:S * p + S, :], b.of(mask).rearrange("a s -> s a"), allow_slow_non_contiguous=True)\
                            .then_inc(in_m[p], 16)
                        sp.dma_start(mrow_u[p][:, :], b.of(mask).broadcast_to([3, S])).then_inc(in_m[p], 16)
                    if name in ("A.w0", "A.w1", "A.w2"):
                        part = int(name[-1])
                        img = scratch[p]
                        main = ((a_hi, hi), (a_mid, mid), (a_lo, lo))[part]
                        side = ((a_ehi, ehi), (a_emid, emid), (a_elo, elo))[part]
                        wait(sp, main[0], b.at(1, 1))
                        for i in range(SLOTS):
                            if Q_PARTS[i] == part:
                                sp.dma_start(img[0][i].rearrange("d h c -> h d c"), main[1][:, 0:T]).then_inc(a_out[p], 16)
                            if K_PARTS[i] == part:
                                sp.dma_start(img[1][i].rearrange("d h c -> h d c"), main[1][:, T:2 * T]).then_inc(a_out[p], 16)
                        wait(sp, side[0], b.at(1, 1))
                        for i in range(SLOTS):
                            if K_PARTS[i] == part:
                                sp.dma_start(img[2][i].rearrange("d h c -> h d c")[:, :, 0:S], side[1][:, :]).then_inc(a_out[p], 16)
                    if name == "A.rd":
                        sp.wait_ge(a_out[p], b.same(18 * 16, 18 * 16))
                        qi, ki, ei = (scratch[p][n].rearrange("i d h c -> (i d) h c") for n in range(3))
                        for e in range(2):
                            r = slice(64 * e, 64 * e + KR)
                            for k in range(NJ):
                                block_at = W * (NJ * e + k)
                                sp.dma_start(qst[p][r, :, k, e, :], qi[:, :, block_at:block_at + W]).then_inc(a_st[p], 16)
                            if e == 0:
                                sp.dma_start(kst[p][r, :, W:T], ki[:, :, 0:T - W]).then_inc(a_st[p], 16)
                            else:
                                sp.dma_start(kst[p][r, :, :], ki[:, :, :]).then_inc(a_st[p], 16)
                            sp.dma_start(est[p][r, :, :], ei[:, :, 0:S]).then_inc(a_st[p], 16)
                    if name == "K.vo":
                        drained(sp, ring_drained, st if p == 0 else st.last, "P.v3", j)
                        for e in range(2):
                            sp.dma_start(vo[p][S * e:S * e + S, :, :], vpair[S * p:S * p + S, e, :, :]).then_inc(k_vo[p], 16)
                    if name == "C.fin":
                        sp.wait_ge(c_yo, b.tile(1, j, 1))
                        dst = b.of(out)[:, 128 * j:128 * j + 128, :].rearrange("a t c -> t (a c)")
                        sp.dma_start(dst, yo[:, j, :]).then_inc(c_out[j], 16)

            run_steps(sp, emit)
            for j in range(NJ):
                sp.wait_ge(c_out[j], 16 * NB)

        @block.tensor
        def _(pe):
            mm = nc.tensor.matmul
            tr = nc.tensor.transpose

            pe.wait_ge(loaded_w, n_w[0])
            pe.wait_ge(consts, 6)
            mm(ring[:, 0, 0:128], kfT[:, :, :].rearrange("f h d -> f (h d)"), qfT[:, :, :].rearrange("f h d -> f (h d)"),
               start=True, stop=True)
            tr(ring[:, 1, 0:128], wkv_s[:, 0:D], ident[:, :]).then_inc(prep_pe, 1)
            pe.wait_ge(prep_ev, 2)
            mm(ring[:, 0, 0:128], wkT[:, :], bd[:, :], start=True, stop=True).then_inc(prep_pe, 1)
            for i in range(2):
                for k in range(4):
                    last = tr(ring[:, 2 + i, 128 * k:128 * k + 128], w1v_s[:, 128 * (4 * i + k):128 * (4 * i + k) + 128],
                              ident[:, :])
                last.then_inc(prep_pe, 1)
            pe.wait_ge(prep_ev, 5)
            for n in range(4):
                e, i = n // 2, n % 2
                for k in range(4):
                    r = slice(64 * e, 64 * e + 64)
                    last = mm(ring[:, 4 + n % 2 if n < 2 else n, 128 * k:128 * k + 128],
                              wvT[r, 4 * i + k, :], w1o_s[r, 4 * i + k, :], start=True, stop=True)
                last.then_inc(prep_pe, 1)
            pe.wait_ge(prep_ev, 9)
            pe.wait_ge(cleared, 18)

            def emit(st):
                for name, j in ORDER:
                    b = stage_of(st, name)
                    if b is None:
                        continue
                    p = b.p
                    bank = None
                    if (name, j) in RING:
                        bank, fill = st.ring(name, j)
                        wait(pe, ring_drained[bank], fill - 1)
                        r = ring[:, bank, :]

                    if name == "A.xT":
                        pe.wait_ge(a_xs, b.at(2, 2))
                        pe.wait_ge(in_a[p], b.same(32, 32))
                        for k in range(NJ):
                            tr(r[:, 128 * k:128 * k + 128], xs[:, k, :], ident[:, :])
                        tr(r[:, 256:256 + S], ca[p][:, :], ident[0:S, 0:S]).then_inc(ring_filled[bank], 1)
                    if name == "A.qk":
                        pe.wait_ge(a_xnT, b.at(1, 1))
                        xq = xnT[p][:, W:W + T].rearrange("c (j e t) -> c e j t", e=2, t=W)
                        mm(r[:, 0:T], wq_s[:, :], xq, start=True, stop=True)
                        mm(r[:, T:2 * T], wwin_s[:, 0:D], xnT[p][:, W:W + T], start=True, stop=True)\
                            .then_inc(ring_filled[bank], 1)
                    if name == "A.vw":
                        pe.wait_ge(a_xnT, b.at(1, 1))
                        for n in range(4):
                            last = mm(r[:, 128 * n:128 * n + 128], xnT[p][:, W * n:W * n + 128], wwin_s[:, D:2 * D],
                                      start=True, stop=True)
                        last.then_inc(ring_filled[bank], 1)
                    if name == "A.enc":
                        drained(pe, ring_drained, st, "A.xT", j, own=bank)
                        c2 = ctxT[p][:, :, :].rearrange("c a s -> c (a s)")
                        mm(r[:, 0:S], wkf_s[:, :], c2[:, 0:S], start=True, stop=True)
                        mm(r[:, S:S + D], c2, wkv_s[:, D:2 * D], start=True, stop=True).then_inc(ring_filled[bank], 1)

                    if name in ("P.k0", "P.k1"):
                        i = int(name[-1])
                        drained(pe, ring_drained, st, "A.xT", 0, own=bank)
                        mm(r, ctxP[:, :, :].rearrange("c a s -> c (a s)"), w1k_s[:, 512 * i:512 * i + 512], start=True, stop=True)\
                            .then_inc(ring_filled[bank], 1)
                    if name in ("P.v0", "P.v1", "P.v2", "P.v3"):
                        n = int(name[-1])
                        e, i = n // 2, n % 2
                        if n == 0:
                            drained(pe, ring_drained, st, "A.xT", 0, own=bank)
                        mm(r, ctxP[:, :, :].rearrange("c a s -> c (a s)"),
                           wvo[:, e, 4 * i:4 * i + 4, :].rearrange("c k n -> c (k n)"), start=True, stop=True)\
                            .then_inc(ring_filled[bank], 1)
                    if name == "K.kT":
                        pe.wait_ge(k_kr, b.same(2, 2))
                        rows = slice(S * p, S * p + S)
                        mm(r[:, 0:S], kr[rows, 0, 0:128], ident[rows, rows], start=True, stop=True)
                        for k in range(1, PAIRS):
                            last = tr(r[:, S * k:S * k + S], kr[rows, k // 4, 128 * (k % 4):128 * (k % 4) + 128], ident[rows, rows])
                        last.then_inc(ring_filled[bank], 1)

                    if name in ("B.s0", "B.s1", "B.s2", "B.s3"):
                        g = int(name[-1])
                        if g == 0 and j == 0:
                            pe.wait_ge(a_st[p], b.same(128, 128))
                        mm(r, ident4[:, 0, :], window[:, j, :, :].rearrange("t h r -> t (h r)"), start=True, stop=False)
                        for k in range(4):
                            h = 4 * g + k
                            last = mm(r[:, 128 * k:128 * k + 128], qst[p][0:KS, h, j, :, :].rearrange("r e t -> r (e t)"),
                                      kst[p][0:KS, h, 128 * j:128 * j + 128], start=False, stop=k == 3)
                        last.then_inc(ring_filled[bank], 1)
                    if name in ("B.lin0", "B.lin1"):
                        i = int(name[-1])
                        if i == 0 and j == 0:
                            pe.wait_ge(a_st[p], b.same(128, 128))
                        for k in range(4):
                            for e in range(2):
                                h = 2 * (4 * i + k) + e
                                last = mm(r[64 * e:64 * e + 64, 128 * k:128 * k + 128], est[p][0:KS, h, :],
                                          qst[p][0:KS, h, j, :, :].rearrange("r e t -> r (e t)"), start=True, stop=True)
                        last.then_inc(ring_filled[bank], 1)
                    if name in ("B.t0", "B.t1", "B.t2", "B.t3"):
                        g = int(name[-1])
                        pe.wait_ge(b_exp, b.tile(4, j, g + 1))
                        for k in range(4):
                            last = tr(r[:, 128 * k:128 * k + 128], pw[:, 4 * g + k, :], ident[:, :])
                        last.then_inc(ring_filled[bank], 1)
                    if name in ("B.pv0", "B.pv1", "B.pv2", "B.pv3"):
                        g = int(name[-1])
                        if g == 0:
                            wait(pe, b_comb, b.tile(3, j, 0))
                        drained(pe, ring_drained, st, f"B.t{g}", j)
                        for k in range(4):
                            h = 4 * g + k
                            last = mm(po[:, NVO * h:NVO * h + NVO], pt[:, h, :], vw[p][:, j, h, :, :].rearrange("r e d -> r (e d)"),
                                      start=True, stop=True)
                        last.then_inc(b_pv, 1)
                    if name == "B.lpv":
                        drained(pe, ring_drained, st, "B.lin1", j)
                        for k in range(PAIRS):
                            c = NVO * (H0 + k)
                            last = mm(po[:, c:c + NVO], wt[:, k, :], vbd[p][:, k, :], start=True, stop=True)
                        last.then_inc(b_pv, 1)
                    if name == "B.cT":
                        pe.wait_ge(b_comb, b.tile(3, j, 3))
                        for k in range(2):
                            last = tr(r[:, 128 * k:128 * k + 128], comb[:, k, :], ident[:, :])
                        last.then_inc(ring_filled[bank], 1)
                    if name == "B.op":
                        drained(pe, ring_drained, st, "B.cT", j, own=bank)
                        for k in range(2):
                            last = mm(r[:, 0:128], combT[:, k, :], wout_s[:, k, :], start=k == 0, stop=k == 1)
                        last.then_inc(ring_filled[bank], 1)
                    if name == "B.xT":
                        drained(pe, ring_drained, st, "B.op", j, own=bank)
                        tr(r[:, 0:128], x1[p][:, j, :], ident[:, :]).then_inc(ring_filled[bank], 1)

                    if name in ("C.q0", "C.q1"):
                        i = int(name[-1])
                        drained(pe, ring_drained, st.last, "B.xT", j, own=bank)
                        mm(r, x1T[p][:, j, :], w1q_s[:, 512 * i:512 * i + 512], start=True, stop=True)\
                            .then_inc(ring_filled[bank], 1)
                    if name in ("C.t0", "C.t1"):
                        i = int(name[-1])
                        pe.wait_ge(c_qr, b.tile(2, j, i + 1))
                        for k in range(4):
                            last = tr(r[:, 128 * k:128 * k + 128], qr[:, i, 128 * k:128 * k + 128], ident[:, :])
                        last.then_inc(ring_filled[bank], 1)
                    if name in ("C.s0", "C.s1"):
                        i = int(name[-1])
                        if i == 0 and j == 0:
                            pe.wait_ge(k_mrow, b.at(1, 1))
                        drained(pe, ring_drained, st, f"C.t{i}", j, own=bank)
                        masked = mrow[p][:, :].rearrange("k (a s) -> k a s", a=1).broadcast_to([3, 8, S])
                        mm(r, ones3[:, :], masked, start=True, stop=False)
                        for k in range(4):
                            last = mm(r[:, 128 * k:128 * k + 128], qT[:, i, k, :], kbd[p][:, 4 * i + k, :],
                                      start=False, stop=k == 3)
                        last.then_inc(ring_filled[bank], 1)
                    if name in ("C.p0", "C.p1"):
                        i = int(name[-1])
                        pe.wait_ge(c_pn, b.tile(2, j, i + 1))
                        for k in range(4):
                            last = tr(r[:, 128 * k:128 * k + 128], pn[:, i, 128 * k:128 * k + 128], ident[:, :])
                        last.then_inc(ring_filled[bank], 1)
                    if name == "C.y":
                        if j == 0:
                            pe.wait_ge(k_vo[p], b.same(32, 32))
                        drained(pe, ring_drained, st, "C.p1", j, own=bank)
                        for k in range(PAIRS):
                            last = mm(r[:, 0:128], pT[:, k // 4, k % 4, :], vo[p][:, k, :], start=k == 0, stop=k == PAIRS - 1)
                        last.then_inc(ring_filled[bank], 1)

            run_steps(pe, emit)

        @block.scalar
        def _(act):
            cp = nc.scalar.copy
            act.wait_ge(loaded_w, n_w[0])
            act.wait_ge(prep_pe, 1)
            cp(wkT[:, :], ring[:, 1, 0:128]).then_inc(prep_ev, 1)
            act.wait_ge(prep_pe, 2)
            cp(wkf_s[:, :], ring[:, 0, 0:128]).then_inc(prep_ev, 1)
            for i in range(2):
                act.wait_ge(prep_pe, 3 + i)
                cp(wvT[:, 4 * i:4 * i + 4, :].rearrange("p k n -> p (k n)"), ring[:, 2 + i, :]).then_inc(prep_ev, 1)
            for n in range(4):
                e, i = n // 2, n % 2
                act.wait_ge(prep_pe, 5 + n)
                cp(wvo[:, e, 4 * i:4 * i + 4, :].rearrange("p k n -> p (k n)"), ring[:, 4 + n if n < 2 else n, :])\
                    .then_inc(prep_ev, 1)

            def emit(st):
                for name, j in ORDER:
                    b = stage_of(st, name)
                    if b is None:
                        continue
                    p = b.p
                    if (name, j) in RING:
                        bank, fill = st.ring(name, j)
                        r = ring[:, bank, :]

                    if name == "L.norm":
                        act.wait_ge(in_a[p], b.same(32, 32))
                        wait(act, a_ms, b.at(1, 0))
                        for k in range(NJ):
                            wait(act, a_ssq, b.at(2, k))
                            nc.scalar.activation(junk[:, :], xa[p][:, k, :], ACT.Square, accum_out=ssq[:, k:k + 1])\
                                .then_inc(a_ssq, 1)
                    if name == "A.qk":
                        act.wait_ge(ring_filled[bank], fill)
                        wait(act, a_out[1 - p], b.before(18 * 16))
                        wait(act, b_pv, b.at(5 * NJ, 5 * NJ) - 10 * NJ)
                        cp(hi[:, :], r).then_inc(a_hi, 1)
                    if name == "A.mid":
                        drained(act, ring_drained, st, "A.qk", 0)
                        cp(mid[:, :], rest[:, :]).then_inc(a_mid, 1)
                    if name == "A.vw":
                        act.wait_ge(ring_filled[bank], fill)
                        for k in range(NJ):
                            last = cp(vw[p][:, k, :, :, 0:HD0].rearrange("r h e d -> r e h d"),
                                      r[:, 256 * k:256 * k + 256].rearrange("r (e h d) -> r e h d", e=2, d=HD0))
                        last.then_inc(ring_drained[bank], 1)
                    if name == "A.enc":
                        act.wait_ge(ring_filled[bank], fill)
                        cp(ehi[:, :], r[:, 0:S]).then_inc(a_ehi, 1)
                    if name == "A.emid":
                        act.wait_ge(a_erest, b.at(1, 1))
                        cp(emid[:, :], erest[:, :]).then_inc(a_emid, 1)
                    if name == "K.kT":
                        act.wait_ge(ring_filled[bank], fill)
                        for e in range(2):
                            q = slice(64 * e, 64 * e + 64)
                            last = cp(kbd[p][q, :, q], r[q, :].rearrange("d (k s) -> d k s", s=S))
                        last.then_inc(ring_drained[bank], 1)
                    if name in ("P.v0", "P.v1", "P.v2", "P.v3"):
                        n = int(name[-1])
                        e, i = n // 2, n % 2
                        act.wait_ge(ring_filled[bank], fill)
                        for q in range(2):
                            wait(act, k_vo[q], b.same(32, 0))
                        last = cp(vpair[:, e, 4 * i:4 * i + 4, :].rearrange("s k n -> s (k n)"), r)
                        last.then_inc(ring_drained[bank], 1)

                    if name in ("B.lin0", "B.lin1"):
                        i = int(name[-1])
                        act.wait_ge(ring_filled[bank], fill)
                        wait(act, b_pv, b.tile(5, j, 0))
                        last = nc.scalar.activation(wt[:, 4 * i:4 * i + 4, :].rearrange("s k t -> s (k t)"), r, ACT.Square,
                                                    bias=ones_col[:, :], scale=0.5)
                        last.then_inc(ring_drained[bank], 1)
                    if name in ("B.e0", "B.e1", "B.e2", "B.e3"):
                        g = int(name[-1])
                        drained(act, ring_drained, st, f"B.s{g}", j)
                        nc.scalar.activation(pw[:, 4 * g:4 * g + 4, :], pw[:, 4 * g:4 * g + 4, :], ACT.Exp,
                                             scale=float(HD0) ** -0.5).then_inc(b_exp, 1)
                    if name in ("B.t0", "B.t1", "B.t2", "B.t3"):
                        g = int(name[-1])
                        act.wait_ge(ring_filled[bank], fill)
                        last = cp(pt[:, 4 * g:4 * g + 4, :].rearrange("r h t -> r (h t)"), r)
                        last.then_inc(ring_drained[bank], 1)
                    if name == "B.cT":
                        act.wait_ge(ring_filled[bank], fill)
                        last = cp(combT[:, :, :].rearrange("c k t -> c (k t)"), r[:, 0:256])
                        last.then_inc(ring_drained[bank], 1)
                    if name == "B.xT":
                        act.wait_ge(ring_filled[bank], fill)
                        last = cp(x1T[p][:, j, :], r[:, 0:128])
                        last.then_inc(ring_drained[bank], 1)

                    if name in ("C.t0", "C.t1"):
                        i = int(name[-1])
                        act.wait_ge(ring_filled[bank], fill)
                        cp(qT[:, i, :, :].rearrange("d k t -> d (k t)"), r).then_inc(ring_drained[bank], 1)
                    if name in ("C.e0", "C.e1"):
                        i = int(name[-1])
                        drained(act, ring_drained, st, f"C.s{i}", j)
                        nc.scalar.activation(pex[:, i, :], pex[:, i, :], ACT.Exp, scale=HD1 ** -0.5).then_inc(c_exp, 1)
                    if name in ("C.p0", "C.p1"):
                        i = int(name[-1])
                        act.wait_ge(ring_filled[bank], fill)
                        cp(pT[:, i, :, :].rearrange("s k t -> s (k t)"), r).then_inc(ring_drained[bank], 1)

            act.wait_ge(consts, 7)
            run_steps(act, emit)

        @block.vector
        def _(dve):
            v = nc.vector
            dve.wait_ge(loaded_w, n_w[0])
            for k in range(4):
                last = v.tensor_copy(ident4[:, k, :], ident[:, :])
            last.then_inc(consts, 1)
            for k in range(4):
                last = v.tensor_copy(window[:, :, k, :], window_f[:, :, :])
            last.then_inc(consts, 1)
            v.memset(ones3[:, :], 1.0).then_inc(consts, 1)
            v.memset(minus_half[:, :], -0.5).then_inc(consts, 1)
            v.tensor_copy(qfT[:, 1:H0, :], qfT[:, 0:1, :].broadcast_to([FD, H0 - 1, HD0])).then_inc(consts, 1)
            v.tensor_copy(kfT[:, 1:H0, :], kfT[:, 0:1, :].broadcast_to([FD, H0 - 1, HD0])).then_inc(consts, 1)
            v.memset(ones_col[:, :], 1.0).then_inc(consts, 1)
            dve.wait_ge(prep_pe, 1)
            v.tensor_tensor(out=bd[:, :], in0=ring[:, 0, 0:128], in1=blocks[:, :], op=ALU.mult).then_inc(prep_ev, 1)

            def rope(dst_a, dst_b, src, cos, sin, n, done):
                heads_n = src.shape[-1] // HD1
                v.tensor_tensor(out=dst_a.rearrange("t (h d) -> t h d", d=HD1), in0=src.rearrange("t (h d) -> t h d", d=HD1),
                                in1=cos.broadcast_to([n, heads_n, HD1]), op=ALU.mult)
                s4 = src.rearrange("t (h i two) -> t h i two", two=2, i=HD1 // 2)
                d4 = dst_b.rearrange("t (h i two) -> t h i two", two=2, i=HD1 // 2)
                c4 = sin.rearrange("t a (i two) -> t a i two", two=2)
                for e in range(2):
                    last = v.tensor_tensor(out=d4[:, :, :, e], in0=s4[:, :, :, 1 - e],
                                           in1=c4[:, :, :, e].broadcast_to([n, heads_n, HD1 // 2]), op=ALU.mult)
                last.then_inc(done, 1)

            def emit(st):
                for name, j in ORDER:
                    b = stage_of(st, name)
                    if b is None:
                        continue
                    p = b.p
                    if (name, j) in RING:
                        bank, fill = st.ring(name, j)
                        r = ring[:, bank, :]

                    if name == "L.norm":
                        dve.wait_ge(a_ssq, b.at(2, 2))
                        v.tensor_scalar(ms[:, :], ssq[:, :], 1.0 / D, 1e-6, ALU.mult, ALU.add).then_inc(a_ms, 1)
                        dve.wait_ge(a_rstd, b.at(1, 1))
                        for k in range(NJ):
                            v.tensor_scalar(xs[:, k, :], xa[p][:, k, :], rstd0[:, k:k + 1], None, ALU.mult).then_inc(a_xs, 1)
                    if name == "A.xT":
                        dve.wait_ge(ring_filled[bank], fill)
                        v.tensor_scalar(xnT[p][:, W:W + T], r[:, 0:T], nw_s[:, :], None, ALU.mult).then_inc(a_xnT, 1)
                        v.tensor_copy(ctxP[:, p, :], r[:, T:T + S])
                        last = v.tensor_copy(ctxT[p][:, :, :], r[:, T:T + S].rearrange("c (a s) -> c a s", a=1).broadcast_to([D, 2, S]))
                        last.then_inc(ring_drained[bank], 1)
                    if name == "A.rest":
                        bank, fill = st.ring("A.qk", j)
                        dve.wait_ge(a_hi, b.at(1, 1))
                        wait(dve, a_lo, b.at(1, 0))
                        last = v.tensor_tensor(out=rest[:, :], in0=ring[:, bank, :], in1=hi[:, :], op=ALU.subtract)
                        last.then_inc(ring_drained[bank], 1)
                    if name == "A.lo":
                        dve.wait_ge(a_mid, b.at(1, 1))
                        v.tensor_tensor(out=lo[:, :], in0=rest[:, :], in1=mid[:, :], op=ALU.subtract).then_inc(a_lo, 1)
                    if name == "A.enc":
                        dve.wait_ge(a_ehi, b.at(1, 1))
                        wait(dve, a_elo, b.at(1, 0))
                        v.tensor_tensor(out=erest[:, :], in0=r[:, 0:S], in1=ehi[:, :], op=ALU.subtract).then_inc(a_erest, 1)
                        for e in range(2):
                            q = slice(64 * e, 64 * e + 64)
                            src = r[q, S:S + D].rearrange("s (k e d) -> s k e d", e=2, d=HD0)
                            last = v.tensor_copy(vbd[p][q, :, 9 * e:9 * e + HD0], src[:, :, e, :])
                        last.then_inc(ring_drained[bank], 1)
                    if name == "A.elo":
                        dve.wait_ge(a_emid, b.at(1, 1))
                        v.tensor_tensor(out=elo[:, :], in0=erest[:, :], in1=emid[:, :], op=ALU.subtract).then_inc(a_elo, 1)

                    if name in ("P.k0", "P.k1"):
                        i = int(name[-1])
                        if i == 0:
                            for q in range(2):
                                dve.wait_ge(in_m[q], b.same(32, 32))
                            v.tensor_scalar(coskm[:, :], cosk[:, :], mcol[:, :], None, ALU.mult).then_inc(k_cos, 1)
                            v.tensor_scalar(sinkm[:, :], sink[:, :], mcol[:, :], None, ALU.mult).then_inc(k_cos, 1)
                            dve.wait_ge(k_cos, b.same(2, 2))
                            wait(dve, k_kr, b.same(2, 0))
                        dve.wait_ge(ring_filled[bank], fill)
                        one = "s (a d) -> s a d"
                        rope(ka[:, i, :], kb[:, i, :], r, coskm[:, :].rearrange(one, a=1),
                             sinkm[:, :].rearrange(one, a=1), 128, ring_drained[bank])
                    if name == "K.kT":
                        dve.wait_ge(in_m[p], b.same(32, 32))
                        v.tensor_scalar(mrow[p][:, :], mrow_u[p][:, :], -1.0, big3[:, :], ALU.add, ALU.mult).then_inc(k_mrow, 1)

                    if name in ("B.s0", "B.s1", "B.s2", "B.s3"):
                        g = int(name[-1])
                        dve.wait_ge(ring_filled[bank], fill)
                        v.tensor_reduce(out=mx[:, 4 * g:4 * g + 4], in_=r.rearrange("t (h r) -> t h r", r=128),
                                        axis=AX.X, op=ALU.max).then_inc(b_max, 1)
                    if name in ("B.d0", "B.d1", "B.d2", "B.d3"):
                        g = int(name[-1])
                        bank, _ = st.ring(f"B.s{g}", j)
                        dve.wait_ge(b_max, b.tile(4, j, g + 1))
                        top = mx[:, 4 * g:4 * g + 4].rearrange("t (h a) -> t h a", a=1).broadcast_to([128, 4, 128])
                        last = v.tensor_tensor(out=pw[:, 4 * g:4 * g + 4, :], in0=ring[:, bank, :].rearrange("t (h r) -> t h r", r=128),
                                               in1=top, op=ALU.subtract)
                        last.then_inc(ring_drained[bank], 1)
                    if name == "B.norm":
                        dve.wait_ge(b_pv, b.tile(5, j, 5))
                        lin = po[:, NVO * H0:NVO * (H0 + PAIRS)].rearrange("t (h d) -> t h d", d=HD0 + 1)
                        win = po[:, 0:NVO * H0].rearrange("t (h d) -> t h d", d=NVO)
                        v.tensor_scalar(den[:, 0, :], lin[:, :, HD0], 1e-6, None, ALU.add)
                        for e in range(2):
                            q = slice(64 * e, 64 * e + 64)
                            last = v.tensor_copy(den[q, 1, :], win[q, :, 9 * e + HD0])
                        last.then_inc(b_den, 1)
                        dve.wait_ge(b_den, b.tile(2, j, 1))
                        v.reciprocal(rden[:, :, :], den[:, :, :]).then_inc(b_den, 1)
                        dve.wait_ge(b_den, b.tile(2, j, 2))
                        v.tensor_tensor(out=comb[:, 0, :].rearrange("t (h d) -> t h d", d=HD0), in0=lin[:, :, 0:HD0],
                                        in1=rden[:, 0, :].rearrange("t (h a) -> t h a", a=1).broadcast_to([128, H0, HD0]),
                                        op=ALU.mult).then_inc(b_comb, 1)
                        for e in range(2):
                            q = slice(64 * e, 64 * e + 64)
                            v.tensor_tensor(out=comb[q, 1, :].rearrange("t (h d) -> t h d", d=HD0),
                                            in0=win[q, :, 9 * e:9 * e + HD0],
                                            in1=rden[q, 1, :].rearrange("t (h a) -> t h a", a=1).broadcast_to([64, H0, HD0]),
                                            op=ALU.mult).then_inc(b_comb, 1)
                    if name == "B.op":
                        dve.wait_ge(ring_filled[bank], fill)
                        dve.wait_ge(in_r[p], b.same(16, 16))
                        last = v.tensor_tensor(out=x1[p][:, j, :], in0=r[:, 0:128], in1=xr[p][:, j, :], op=ALU.add)
                        last.then_inc(ring_drained[bank], 1)

                    if name in ("C.q0", "C.q1"):
                        i = int(name[-1])
                        dve.wait_ge(ring_filled[bank], fill)
                        wait(dve, c_qr, b.tile(2, j, i + 1) - 2)
                        rope(qa[:, i, :], qb[:, i, :], r, cosq[:, j:j + 1, :], sinq[:, j:j + 1, :], 128, ring_drained[bank])
                    if name in ("C.s0", "C.s1"):
                        i = int(name[-1])
                        dve.wait_ge(ring_filled[bank], fill)
                        wait(dve, c_pn, b.tile(2, j, i + 1) - 2)
                        v.tensor_reduce(out=mx1[:, 8 * i:8 * i + 8], in_=r.rearrange("t (h s) -> t h s", s=S),
                                        axis=AX.X, op=ALU.max).then_inc(c_max, 1)
                    if name in ("C.d0", "C.d1"):
                        i = int(name[-1])
                        bank, _ = st.ring(f"C.s{i}", j)
                        dve.wait_ge(c_max, b.tile(2, j, i + 1))
                        top = mx1[:, 8 * i:8 * i + 8].rearrange("t (h a) -> t h a", a=1).broadcast_to([128, 8, S])
                        v.tensor_tensor(out=pex[:, i, :].rearrange("t (h s) -> t h s", s=S),
                                        in0=ring[:, bank, :].rearrange("t (h s) -> t h s", s=S), in1=top,
                                        op=ALU.subtract).then_inc(ring_drained[bank], 1)
                    if name in ("C.n0", "C.n1"):
                        i = int(name[-1])
                        q = slice(8 * i, 8 * i + 8)
                        dve.wait_ge(c_exp, b.tile(2, j, i + 1))
                        v.tensor_reduce(out=lsum[:, q], in_=pex[:, i, :].rearrange("t (h s) -> t h s", s=S), axis=AX.X,
                                        op=ALU.add).then_inc(c_sum, 1)
                        dve.wait_ge(c_sum, b.tile(2, j, i + 1))
                        v.reciprocal(rsum[:, q], lsum[:, q]).then_inc(c_rsum, 1)
                    if name == "C.y":
                        dve.wait_ge(ring_filled[bank], fill)
                        wait(dve, c_zn, b.tile(1, j, 0))
                        v.tensor_tensor(out=z[:, :], in0=r[:, 0:128], in1=x1[p][:, j, :], op=ALU.add)\
                            .then_inc(c_z, 1)
                        dve.wait_ge(c_z, b.tile(1, j, 1))
                        v.bn_stats(stats[:, :], z[:, :]).then_inc(ring_drained[bank], 1)
                        dve.wait_ge(loaded_w, n_w[0])
                        dve.wait_ge(ring_drained[bank], fill)
                        v.bn_aggr(mv[:, :], stats[:, :]).then_inc(c_var, 1)
                        dve.wait_ge(c_var, b.tile(1, j, 1))
                        v.tensor_scalar(veps[:, :], mv[:, 1:2], 1e-3, None, ALU.add).then_inc(c_veps, 1)
                    if name == "C.fin":
                        dve.wait_ge(c_rstd, b.tile(1, j, 1))
                        wait(dve, c_zg, b.tile(1, j, 0))
                        v.tensor_scalar(zn[:, :], z[:, :], mv[:, 0:1], rstd1[:, :], ALU.subtract, ALU.mult).then_inc(c_zn, 1)

            run_steps(dve, emit)

        @block.gpsimd
        def _(pool):
            g = nc.gpsimd
            n = 0
            for p in range(2):
                for part, value in ((qst[p][:, :, :, :, :], 0.0), (kst[p][:, :, :], 0.0),
                                    (est[p][:, :, :], 0.0), (vw[p][:, :, :, :, :], 1.0), (vbd[p][:, :, :], 0.0),
                                    (vbd[p][0:64, :, HD0:HD0 + 1], 1.0), (vbd[p][64:128, :, NVO - 1:NVO], 1.0),
                                    (kbd[p][:, :, :], 0.0), (xnT[p][:, 0:W], 0.0)):
                    wait(pool, cleared, n)
                    g.memset(part, value).then_inc(cleared, 1)
                    n += 1
            pool.wait_ge(cleared, n)
            pool.wait_ge(loaded_w, n_w[0])
            pool.wait_ge(consts, 4)

            def emit(st):
                for name, j in ORDER:
                    b = stage_of(st, name)
                    if b is None:
                        continue
                    p = b.p
                    if name == "L.norm":
                        pool.wait_ge(a_ms, b.at(1, 1))
                        wait(pool, a_xs, b.at(2, 0))
                        g.tensor_tensor(out=rstd0[:, :], in0=ms[:, :], in1=minus_half[:, :], op=ALU.pow).then_inc(a_rstd, 1)
                    if name in ("P.k0", "P.k1"):
                        i = int(name[-1])
                        drained(pool, ring_drained, st, name, j)
                        g.tensor_tensor(out=kr[:, i, :], in0=ka[:, i, :], in1=kb[:, i, :], op=ALU.add).then_inc(k_kr, 1)
                    if name in ("C.q0", "C.q1"):
                        i = int(name[-1])
                        drained(pool, ring_drained, st, name, j)
                        g.tensor_tensor(out=qr[:, i, :], in0=qa[:, i, :], in1=qb[:, i, :], op=ALU.add).then_inc(c_qr, 1)
                    if name in ("C.n0", "C.n1"):
                        i = int(name[-1])
                        pool.wait_ge(c_rsum, b.tile(2, j, i + 1))
                        rs = rsum[:, 8 * i:8 * i + 8].rearrange("t (h a) -> t h a", a=1).broadcast_to([128, 8, S])
                        g.tensor_tensor(out=pn[:, i, :].rearrange("t (h s) -> t h s", s=S),
                                        in0=pex[:, i, :].rearrange("t (h s) -> t h s", s=S), in1=rs, op=ALU.mult)\
                            .then_inc(c_pn, 1)
                    if name == "C.y":
                        pool.wait_ge(c_veps, b.tile(1, j, 1))
                        g.tensor_tensor(out=rstd1[:, :], in0=veps[:, :], in1=minus_half[:, 0:1], op=ALU.pow).then_inc(c_rstd, 1)
                    if name == "C.fin":
                        pool.wait_ge(c_zn, b.tile(1, j, 1))
                        g.tensor_tensor(out=zg[:, :], in0=zn[:, :], in1=gamma_s[:, :], op=ALU.mult).then_inc(c_zg, 1)
                        pool.wait_ge(c_zg, b.tile(1, j, 1))
                        wait(pool, c_out[j], b.at(16, 0))
                        g.tensor_tensor(out=yo[:, j, :], in0=zg[:, :], in1=beta_s[:, :], op=ALU.add).then_inc(c_yo, 1)

            run_steps(pool, emit)


def constants():
    f = np.float32
    t = np.arange(128)
    r = np.arange(128)
    tt, rr = (t % W)[:, None], r[None, :]
    ok = (rr >= tt) & (rr <= tt + W)
    first = ok & ((rr >= W) | (t[:, None] >= W))
    window = np.where(np.stack([first, ok], 1), f(0), f(-1e30)).astype(f)
    blk = np.arange(128) // HD0
    blocks = (blk[:, None] == blk[None, :]).astype(f)
    inv = (f(1.0) / np.power(f(10000.0), np.arange(0, HD1, 2, dtype=f) / f(HD1))).astype(f)
    ang = (np.arange(T, dtype=f)[:, None] * inv[None, :]).astype(f)
    cos, sin = np.cos(ang).astype(f), np.sin(ang).astype(f)
    rope = np.stack([np.repeat(cos, 2, 1), np.stack([-sin, sin], -1).reshape(T, HD1)]).astype(f)
    left, big = f(BIG), []
    for _ in range(3):
        top = (left.view(np.uint32) & np.uint32(0xFFFF0000)).view(f)
        big.append(top)
        left = f(left - top)
    return {"tab_ident": np.eye(128, dtype=f), "tab_window": window, "tab_blocks": blocks, "tab_rope": rope,
            "tab_big": np.array(big, f).reshape(3, 1)}


_INS = ["x", "ctx_1024", "mask_BxS2_bf1", "L0_xattn_norm_w", "L0_xattn_Wq", "L0_xattn_Wkv", "L0_xattn_Wqf",
        "L0_xattn_Wkf", "L0_xattn_Wwin", "L0_xattn_Wout", "L1_xattn_Wq", "L1_xattn_Wk", "L1_xattn_Wv", "L1_xattn_Wo",
        "L1_xattn_ln_gamma", "L1_xattn_ln_beta"]


def kernel(**inputs):
    import concourse.bacc as bacc
    from concourse.bass_utils import run_bass_kernel_spmd

    nc = bacc.Bacc("TRN2", target_bir_lowering=False, num_devices=1)
    arrays, args = {}, []
    for name in _INS:
        a = np.ascontiguousarray(inputs[name])
        if a.dtype == np.bool_:
            a = a.view(np.uint8)
        if name in ("L0_xattn_Wqf", "L0_xattn_Wkf"):
            a = np.ascontiguousarray(a.T)
        arrays["in_" + name] = a
        args.append(nc.dram_tensor("in_" + name, a.shape, mybir.dt.from_np(a.dtype), kind="ExternalInput").ap())
    for name, a in constants().items():
        arrays[name] = a
        args.append(nc.dram_tensor(name, a.shape, F32, kind="ExternalInput").ap())
    out = nc.dram_tensor("out_0", (NB, T, D), F32, kind="ExternalOutput").ap()
    scratch = [[nc.dram_tensor(f"stack{p}_{n}", (SLOTS, HD0, H0, T), BF16, kind="Internal").ap() for n in range(3)]
               for p in range(2)]
    build(nc, *args, out, scratch)
    r = run_bass_kernel_spmd(nc, [arrays], core_ids=[0])
    return r.results[0]["out_0"]
```

```python
import concourse.bass as bass
from concourse import mybir
from contextlib import ExitStack
import numpy as np

F32 = mybir.dt.float32
BF16 = mybir.dt.bfloat16
F32R = mybir.dt.float32r
U8 = mybir.dt.uint8
ALU = mybir.AluOpType
ACT = mybir.ActivationFunctionType
AX = mybir.AxisListType

NB, T, D = 16, 256, 128
S = 64
H0, HD0, FD = 16, 8, 16
H1, HD1 = 16, 64
W = 64
PAIRS = 8
NJ = T // 128
SLOTS = 6
KR = SLOTS * HD0
KS = 112
Q_PARTS = (0, 0, 1, 1, 0, 2)
K_PARTS = (0, 1, 0, 1, 2, 0)
BIG = 8e9
NVO = 18


class Batch:

    def __init__(self, half, parity, loop=None):
        self.h, self.p, self.loop = half if loop is None else loop + half, parity, loop
        self.offset = half

    def of(self, array):
        pairs = array.rearrange({2: "(h q) s -> q h s", 3: "(h q) s c -> q h s c"}[len(array.shape)], q=2)[self.p]
        return pairs[bass.ds(self.offset, 1)] if self.loop is None else pairs[self.offset:][bass.ds(self.loop, 1)]

    def at(self, per, k):
        return self.h * (2 * per) + (self.p * per + k)

    def tile(self, per, j, k):
        return self.at(NJ * per, j * per + k)

    def same(self, per, k):
        return self.h * per + k

    def before(self, per):
        return (self.h + self.p) * per


ORDER = [(x.split(":")[0], int(x.split(":")[1])) for x in """
    A.xT:0 C.q0:0 B.lin0:0 B.s0:0 B.d0:0 B.lin1:0 C.q1:0 A.vw:0 P.v0:1 A.qk:0 A.rest:0 B.e0:0 A.enc:0 C.t0:0
    C.q0:1 B.s1:0 B.t0:0 B.d1:0 C.s0:0 C.t1:0 B.s2:0 B.e1:0 B.d2:0 B.pv0:0 B.e2:0 A.emid:0 B.s3:0 C.d0:0 B.d3:0
    C.q1:1 B.t1:0 C.e0:0 B.e3:0 B.lpv:0 B.s0:1 B.t2:0 B.s1:1 C.t0:1 A.elo:0 C.n0:0 B.pv1:0 B.d0:1 B.t3:0 A.w0:0
    C.s1:0 C.d1:0 B.d1:1 B.s2:1 C.e1:0 B.pv2:0 B.e0:1 C.p0:0 B.d2:1 B.e1:1 B.pv3:0 B.e2:1 A.mid:0 C.n1:0 C.s0:1
    C.d0:1 L.load:0 B.lin0:1 C.t1:1 B.t0:1 B.t1:1 B.t2:1 B.norm:0 B.lin1:1 B.s3:1 A.lo:0 C.p1:0 C.e0:1 B.d3:1
    C.s1:1 C.d1:1 C.n0:1 P.k0:0 C.e1:1 C.n1:1 A.load:0 A.w1:0 B.e3:1 B.pv0:1 B.cT:0 A.w2:0 C.y:0 P.v1:1 B.lpv:1
    B.op:0 L.norm:1 P.k1:0 B.t3:1 B.pv1:1 A.rd:0 C.p0:1 C.fin:0 B.pv2:1 C.p1:1 B.xT:0 B.pv3:1 B.norm:1 P.v2:1
    C.y:1 B.cT:1 A.hi:0 K.kT:1 B.op:1 P.v3:1 K.vo:1 C.fin:1 B.xT:1
""".split()]
NRING = 7
RING = [x for x in ORDER if x[0] in (
    "A.xT", "A.qk", "A.vw", "A.enc", "P.k0", "P.k1", "P.v0", "P.v1", "P.v2", "P.v3", "K.kT", "B.s0", "B.s1", "B.s2", "B.s3",
    "B.lin0", "B.lin1", "B.t0", "B.t1", "B.t2", "B.t3", "B.cT", "B.op", "B.xT",
    "C.q0", "C.q1", "C.t0", "C.t1", "C.s0", "C.s1", "C.p0", "C.p1", "C.y")]


def stage_of(step, name):
    if name[0] == "P":
        return step.b if step.b is not None and step.b.p == 0 else None
    return {"L": step.l, "A": step.a, "B": step.b, "K": step.b, "C": step.c}[name[0]]


class Step:

    def __init__(self, stages, filled, last=None):
        self.l, self.a, self.b, self.c = stages
        self.filled, self.last = filled, last

    def ring(self, name, j):
        n = RING.index((name, j))
        bank = n % NRING
        mine = sum(1 for m in range(bank, n + 1, NRING) if stage_of(self, RING[m][0]) is not None)
        return bank, self.filled[bank] + mine

    def fills(self):
        out = [0] * NRING
        for m, (name, _) in enumerate(RING):
            if stage_of(self, name) is not None:
                out[m % NRING] += 1
        return out


PEELED = 4


STAGES = 4


def run_steps(eng, emit, after=None):
    filled, step = [0] * NRING, None

    def plain(s, step, filled):
        stages = [Batch((s - n) // 2, (s - n) % 2) if 0 <= s - n < NB else None for n in range(STAGES)]
        step = Step(stages, filled, step)
        emit(step)
        return step, [x + y for x, y in zip(filled, step.fills())]

    for s in range(PEELED):
        step, filled = plain(s, step, filled)
        if after and s in after:
            after[s](filled)

    def looped(i, p, filled, last=None, back=0):
        stages = [Batch((PEELED + p - n) // 2 - back, (PEELED + p - n) % 2, i) for n in range(STAGES)]
        return Step(stages, filled, last)

    full = [looped(0, p, filled).fills() for p in range(2)]
    per_pair = [x + y for x, y in zip(*full)]
    pairs = (NB - PEELED) // 2
    with eng.Fori(0, pairs) as i:
        even = [i * n + x for n, x in zip(per_pair, filled)]
        odd = [i * n + (x + m) for n, x, m in zip(per_pair, filled, full[0])]
        before = [i * n + (x - m) for n, x, m in zip(per_pair, filled, full[1])]
        emit(looped(i, 0, even, looped(i, 1, before, back=1)))
        emit(looped(i, 1, odd, looped(i, 0, even)))
    filled = [x + pairs * n for x, n in zip(filled, per_pair)]
    step = looped(pairs - 1, 1, [x - n for n, x in zip(full[1], filled)])
    for s in range(NB, NB + STAGES - 1):
        step, filled = plain(s, step, filled)


def drained(eng, sems, step, name, j, own=None):
    bank, fill = step.ring(name, j)
    if bank != own:
        wait(eng, sems[bank], fill)


def wait(eng, sem, value):
    if not isinstance(value, int) or value > 0:
        eng.wait_ge(sem, value)


def build(nc, x, ctx, mask, norm_w, wq, wkv, wqf, wkf, wwin, wout, w1q, w1k, w1v, w1o, gamma, beta,
          tab_ident, tab_window, tab_blocks, tab_rope, tab_big, out, scratch):
    es = ExitStack()
    with es:
        def sb(name, shape, dt=F32):
            return es.enter_context(nc.sbuf_tensor(name, shape, dt))

        def pb(name, shape):
            return es.enter_context(nc.psum_tensor(name, shape, F32))

        def sem(name):
            return es.enter_context(nc.semaphore(name))

        def two(name, shape, dt=F32):
            return [sb(f"{name}{p}", shape, dt) for p in range(2)]

        wq_s, wkv_s, wwin_s = sb("wq_s", [D, D]), sb("wkv_s", [D, 2 * D]), sb("wwin_s", [D, 2 * D])
        wout_s = sb("wout_s", [D, 2, D])
        nw_s = sb("nw_s", [D, 1])
        qfT, kfT = sb("qfT", [FD, H0, HD0]), sb("kfT", [FD, H0, HD0])
        gamma_s, beta_s = sb("gamma_s", [128, D]), sb("beta_s", [128, D])
        ident = sb("ident", [128, 128])
        ident4 = sb("ident4", [128, 4, 128], BF16)
        window_f = sb("window_f", [128, NJ, 128])
        window = sb("window", [128, NJ, 4, 128], BF16)
        blocks = sb("blocks", [128, 128])
        cosq, sinq = sb("cosq", [128, NJ, HD1]), sb("sinq", [128, NJ, HD1])
        big3 = sb("big3", [3, 1])
        ones3 = sb("ones3", [3, 128], BF16)
        minus_half = sb("minus_half", [128, 2])
        ones_col = sb("ones_col", [128, 1])
        bd = sb("bd", [128, 128])
        wkT = sb("wkT", [128, 128])
        wkf_s = sb("wkf_s", [D, D])
        wq_r, wwin_r = sb("wq_r", [D, 2, D]), sb("wwin_r", [D, 2, D])
        w1q_r, w1k_r = sb("w1q_r", [D, 2, H1 * HD1]), sb("w1k_r", [D, 2, H1 * HD1])
        wvo_r = sb("wvo_r", [D, 2, 4, 512])

        xa, ca = two("xa", [128, NJ, D]), two("ca", [S, D])
        xr = two("xr", [128, NJ, D])
        mcol, mrow_u = sb("mcol", [128, 1], U8), two("mrow_u", [3, S], U8)
        junk = sb("junk", [128, D])
        ssq, ms, rstd0 = sb("ssq", [128, NJ]), sb("ms", [128, NJ]), sb("rstd0", [128, NJ])
        xs = sb("xs", [128, NJ, D])
        xnT = two("xnT", [D, W + T])
        ctxT = two("ctxT", [D, 2, S])
        xnU, xnL = sb("xnU", [D, T]), sb("xnL", [D, T])
        ctxU, ctxL = sb("ctxU", [D, 2, S]), sb("ctxL", [D, 2, S])
        hi, mid, lo = sb("hi", [128, 2 * T + S], BF16), sb("mid", [128, 2 * T + S], BF16), sb("lo", [128, 2 * T + S], BF16)
        QK, EN = slice(0, 2 * T), slice(2 * T, 2 * T + S)
        rest = sb("rest", [128, 2 * T])
        erest = sb("erest", [128, S])
        qst = two("qst", [128, H0, NJ, 2, W], BF16)
        kst = two("kst", [128, H0, T + S], BF16)
        vw = two("vw", [128, NJ, H0, 2, HD0 + 1])
        vbd = two("vbd", [128, PAIRS, NVO])

        mx = sb("mx", [128, H0])
        pw = sb("pw", [128, H0, 128])
        wt = sb("wt", [128, PAIRS, 128])
        pt = sb("pt", [128, H0, 128])
        den, rden = sb("den", [128, 2, H0]), sb("rden", [128, 2, H0])
        comb = sb("comb", [128, 2, D])
        combT = sb("combT", [128, 2, 128])
        x1 = two("x1", [128, NJ, D])
        x1U, x1L = two("x1U", [128, NJ, D]), two("x1L", [128, NJ, D])
        cosk, sink = sb("cosk", [128, HD1]), sb("sink", [128, HD1])
        coskm, sinkm = sb("coskm", [128, HD1]), sb("sinkm", [128, HD1])
        ka, kb = sb("ka", [128, 2, 512]), sb("kb", [128, 2, 512])
        vpair = sb("vpair", [128, 2, PAIRS, D])
        kbd = two("kbd", [128, PAIRS, 128])
        vo = two("vo", [128, PAIRS, D])
        mrow = two("mrow", [3, S], BF16)

        qa, qb = sb("qa", [128, 2, 512]), sb("qb", [128, 2, 512])
        qT = sb("qT", [128, 2, 4, 128])
        mx1 = sb("mx1", [128, H1])
        pex = sb("pex", [128, 2, 512])
        lsum, rsum = sb("lsum", [128, H1]), sb("rsum", [128, H1])
        pT = sb("pT", [128, 2, 4, 128])
        z, zn, zg, yo = sb("z", [128, D]), sb("zn", [128, D]), sb("zg", [128, D]), sb("yo", [128, NJ, D])
        stats, mv = sb("stats", [128, 6]), sb("mv", [128, 2])
        veps, rstd1 = sb("veps", [128, 1]), sb("rstd1", [128, 1])

        ring = pb("ring", [128, NRING, 512])
        po = pb("po", [128, 512])

        loaded = [sem(f"loaded{n}") for n in range(3)]
        cleared, stacks_cleared, consts = sem("cleared"), sem("stacks_cleared"), sem("consts")
        prep_pe, prep_ev = sem("prep_pe"), sem("prep_ev")
        w_upper, w_rest = sem("w_upper"), sem("w_rest")
        a_xnU, a_ctxU, b_x1U = sem("a_xnU"), sem("a_ctxU"), sem("b_x1U")
        ring_filled = [sem(f"ring_filled{i}") for i in range(NRING)]
        ring_drained = [sem(f"ring_drained{i}") for i in range(NRING)]
        in_a = [sem(f"in_a{p}") for p in range(2)]
        in_m = [sem(f"in_m{p}") for p in range(2)]
        in_r = [sem(f"in_r{p}") for p in range(2)]
        a_ssq, a_ms, a_rstd, a_xs = sem("a_ssq"), sem("a_ms"), sem("a_rstd"), sem("a_xs")
        a_xnT = sem("a_xnT")
        a_hi, a_mid, a_lo = sem("a_hi"), sem("a_mid"), sem("a_lo")
        a_ehi, a_erest, a_emid, a_elo = sem("a_ehi"), sem("a_erest"), sem("a_emid"), sem("a_elo")
        a_out = [sem(f"a_out{p}") for p in range(2)]
        a_st = [sem(f"a_st{p}") for p in range(2)]
        k_mrow, k_cos, k_kr = sem("k_mrow"), sem("k_cos"), sem("k_kr")
        k_vo = [sem(f"k_vo{p}") for p in range(2)]
        b_max, b_exp, b_pv = sem("b_max"), sem("b_exp"), sem("b_pv")
        b_den, b_comb = sem("b_den"), sem("b_comb")
        c_qr = sem("c_qr")
        c_max, c_exp, c_sum, c_rsum, c_pn = sem("c_max"), sem("c_exp"), sem("c_sum"), sem("c_rsum"), sem("c_pn")
        c_z, c_var, c_veps, c_rstd = (sem(n) for n in ("c_z", "c_var", "c_veps", "c_rstd"))
        c_zn, c_zg, c_yo = sem("c_zn"), sem("c_zg"), sem("c_yo")
        c_out = [sem(f"c_out{j}") for j in range(NJ)]

        block = es.enter_context(nc.Block())
        n_loaded = [0, 0, 0]

        @block.sync
        def _(sp):
            def load(group, dst, src):
                sp.dma_start(dst, src).then_inc(loaded[group], 16)
                n_loaded[group] += 16

            load(0, ident[:, :], tab_ident)
            load(0, qfT[:, 0, :], wqf)
            load(0, kfT[:, 0, :], wkf)
            load(0, blocks[:, :], tab_blocks)
            load(0, wkv_s[:, :], wkv)
            load(0, nw_s[:, :], norm_w.rearrange("(p a) -> p a", a=1))
            load(0, wq_s[:, :], wq)
            load(0, wwin_s[:, :], wwin)
            load(0, window_f[:, :, :], tab_window)

            def load_more(filled):
                load(1, ka[:, :, :], w1v.rearrange("c (a n) -> c a n", a=2))
                load(1, kb[:, :, :].rearrange("p a (k n) -> p (a k) n", n=D), w1o.rearrange("(k p) n -> p k n", p=128))
                load(1, wout_s[:, :, :], wout.rearrange("(k p) n -> p k n", p=128))
                load(1, big3[:, :], tab_big)

            def load_last(filled):
                sp.wait_ge(stacks_cleared, 4)
                load(2, qb[:, :, :], w1k.rearrange("c (a n) -> c a n", a=2))
                for p in range(2):
                    load(2, cosk[S * p:S * p + S, :], tab_rope[0][0:S, :])
                    load(2, sink[S * p:S * p + S, :], tab_rope[1][0:S, :])
                load(2, qa[:, :, :], w1q.rearrange("c (a n) -> c a n", a=2))
                load(2, cosq[:, :, :], tab_rope[0].rearrange("(j t) d -> t j d", t=128))
                load(2, sinq[:, :, :], tab_rope[1].rearrange("(j t) d -> t j d", t=128))
                load(2, gamma_s[:, :], gamma.rearrange("(a n) -> a n", a=1).broadcast_to([128, D]))
                load(2, beta_s[:, :], beta.rearrange("(a n) -> a n", a=1).broadcast_to([128, D]))

            def emit(st):
                for name, j in ORDER:
                    b = stage_of(st, name)
                    if b is None:
                        continue
                    p = b.p
                    if name == "L.load":
                        wait(sp, a_xs, b.at(2, 2) - 4)
                        wait(sp, a_xnT, b.at(1, 1) - 2)
                        sp.dma_start(xa[p][:, :, :], b.of(x).rearrange("a (j t) c -> t (a j) c", t=128)).then_inc(in_a[p], 16)
                        sp.dma_start(ca[p][:, :], b.of(ctx).rearrange("a s c -> s (a c)")).then_inc(in_a[p], 16)
                    if name == "A.load":
                        if st.last is not None and st.last.b is not None:
                            drained(sp, ring_drained, st.last, "B.op", NJ - 1)
                        sp.dma_start(xr[p][:, :, :], b.of(x).rearrange("a (j t) c -> t (a j) c", t=128)).then_inc(in_r[p], 16)
                        sp.dma_start(mcol[S * p:S * p + S, :], b.of(mask).rearrange("a s -> s a"), allow_slow_non_contiguous=True)\
                            .then_inc(in_m[p], 16)
                        sp.dma_start(mrow_u[p][:, :], b.of(mask).broadcast_to([3, S])).then_inc(in_m[p], 16)
                    if name in ("A.w0", "A.w1", "A.w2"):
                        part = int(name[-1])
                        img = scratch[p]
                        tile = (hi, mid, lo)[part]
                        wait(sp, (a_hi, a_mid, a_lo)[part], b.at(1, 1))
                        for i in range(SLOTS):
                            if Q_PARTS[i] == part:
                                sp.dma_start(img[0][i].rearrange("d h c -> h d c")[:, :, 0:T], tile[:, 0:T]).then_inc(a_out[p], 16)
                        wait(sp, (a_ehi, a_emid, a_elo)[part], b.at(1, 1))
                        for i in range(SLOTS):
                            if K_PARTS[i] == part:
                                sp.dma_start(img[1][i].rearrange("d h c -> h d c"), tile[:, T:2 * T + S]).then_inc(a_out[p], 16)
                    if name == "A.rd":
                        sp.wait_ge(stacks_cleared, 2)
                        sp.wait_ge(a_out[p], b.same(12 * 16, 12 * 16))
                        qi, ki = (scratch[p][n].rearrange("i d h c -> (i d) h c") for n in range(2))
                        for e in range(2):
                            r = slice(64 * e, 64 * e + KR)
                            for k in range(NJ):
                                block_at = W * (NJ * e + k)
                                sp.dma_start(qst[p][r, :, k, e, :], qi[:, :, block_at:block_at + W]).then_inc(a_st[p], 16)
                            if e == 0:
                                sp.dma_start(kst[p][r, :, W:T], ki[:, :, 0:T - W]).then_inc(a_st[p], 16)
                                sp.dma_start(kst[p][r, :, T:T + S], ki[:, :, T:T + S]).then_inc(a_st[p], 16)
                            else:
                                sp.dma_start(kst[p][r, :, :], ki[:, :, :]).then_inc(a_st[p], 16)
                    if name == "K.vo":
                        drained(sp, ring_drained, st if p == 0 else st.last, "P.v3", j)
                        for e in range(2):
                            sp.dma_start(vo[p][S * e:S * e + S, :, :], vpair[S * p:S * p + S, e, :, :]).then_inc(k_vo[p], 16)
                    if name == "C.fin":
                        sp.wait_ge(c_yo, b.tile(1, j, 1))
                        dst = b.of(out)[:, 128 * j:128 * j + 128, :].rearrange("a t c -> t (a c)")
                        sp.dma_start(dst, yo[:, j, :]).then_inc(c_out[j], 16)

            run_steps(sp, emit, {0: load_more, 1: load_last})
            for j in range(NJ):
                sp.wait_ge(c_out[j], 16 * NB)

        @block.tensor
        def _(pe):
            mm = nc.tensor.matmul
            tr = nc.tensor.transpose

            def mm3(dst, lhs_u, lhs_l, rhs_u, rhs_l):
                mm(dst, lhs_u.bitcast(F32R), rhs_u.bitcast(F32R), start=True, stop=False)
                mm(dst, lhs_u.bitcast(F32R), rhs_l.bitcast(F32R), start=False, stop=False)
                return mm(dst, lhs_l.bitcast(F32R), rhs_u.bitcast(F32R), start=False, stop=True)

            pe.wait_ge(loaded[0], n_loaded[0])
            pe.wait_ge(consts, 5)
            mm(ring[:, 0, 0:128], kfT[:, :, :].rearrange("f h d -> f (h d)"), qfT[:, :, :].rearrange("f h d -> f (h d)"),
               start=True, stop=True)
            tr(ring[:, 1, 0:128], wkv_s[:, 0:D], ident[:, :]).then_inc(prep_pe, 1)
            pe.wait_ge(prep_ev, 2)
            mm(ring[:, 0, 0:128], wkT[:, :], bd[:, :], start=True, stop=True).then_inc(prep_pe, 1)
            pe.wait_ge(prep_ev, 3)
            pe.wait_ge(w_rest, 2)
            pe.wait_ge(cleared, 12)

            def prepare_values(filled):
                pe.wait_ge(loaded[1], n_loaded[1])
                pe.wait_ge(stacks_cleared, 4)
                pe.wait_ge(consts, 7)
                for bank in range(NRING):
                    wait(pe, ring_drained[bank], filled[bank])
                for i in range(2):
                    for k in range(4):
                        last = tr(ring[:, 2 + i, 128 * k:128 * k + 128], ka[:, i, 128 * k:128 * k + 128],
                                  ident[:, :])
                    last.then_inc(prep_pe, 1)
                pe.wait_ge(prep_ev, 5)
                for n in range(4):
                    e, i = n // 2, n % 2
                    for k in range(4):
                        r = slice(64 * e, 64 * e + 64)
                        last = mm(ring[:, 2 + n, 128 * k:128 * k + 128], pex[r, i, 128 * k:128 * k + 128], kb[r, i, 128 * k:128 * k + 128],
                                  start=True, stop=True)
                    last.then_inc(prep_pe, 1)
                pe.wait_ge(prep_ev, 9)
                pe.wait_ge(w_rest, 6)

            def emit(st):
                for name, j in ORDER:
                    b = stage_of(st, name)
                    if b is None:
                        continue
                    p = b.p
                    bank = None
                    if (name, j) in RING:
                        bank, fill = st.ring(name, j)
                        wait(pe, ring_drained[bank], fill - 1)
                        r = ring[:, bank, :]

                    if name == "A.xT":
                        pe.wait_ge(a_xs, b.at(2, 2))
                        pe.wait_ge(in_a[p], b.same(32, 32))
                        for k in range(NJ):
                            tr(r[:, 128 * k:128 * k + 128], xs[:, k, :], ident[:, :])
                        tr(r[:, 256:256 + S], ca[p][:, :], ident[0:S, 0:S]).then_inc(ring_filled[bank], 1)
                    if name == "A.qk":
                        pe.wait_ge(a_xnT, b.at(1, 1))
                        order = "c (j e t) -> c e j t"
                        mm3(r[:, 0:T], wq_r[:, 0, :], wq_r[:, 1, :], xnU[:, :].rearrange(order, e=2, t=W),
                            xnL[:, :].rearrange(order, e=2, t=W))
                        mm3(r[:, T:2 * T], wwin_r[:, 0, :], wwin_r[:, 1, :], xnU[:, :], xnL[:, :]).then_inc(ring_filled[bank], 1)
                    if name == "A.vw":
                        pe.wait_ge(a_xnT, b.at(1, 1))
                        for n in range(4):
                            last = mm(r[:, 128 * n:128 * n + 128], xnT[p][:, W * n:W * n + 128], wwin_s[:, D:2 * D],
                                      start=True, stop=True)
                        last.then_inc(ring_filled[bank], 1)
                    if name == "A.enc":
                        drained(pe, ring_drained, st, "A.xT", j, own=bank)
                        c2 = ctxT[p][:, :, :].rearrange("c a s -> c (a s)")
                        mm(r[:, 0:S], wkf_s[:, :], c2[:, 0:S], start=True, stop=True)
                        mm(r[:, S:S + D], c2, wkv_s[:, D:2 * D], start=True, stop=True).then_inc(ring_filled[bank], 1)

                    if name in ("P.k0", "P.k1"):
                        i = int(name[-1])
                        if i == 0:
                            pe.wait_ge(loaded[2], n_loaded[2])
                            pe.wait_ge(w_rest, 8)
                        drained(pe, ring_drained, st, "A.xT", 0, own=bank)
                        cols = slice(512 * i, 512 * i + 512)
                        mm3(r, ctxU[:, :, :].rearrange("c a s -> c (a s)"), ctxL[:, :, :].rearrange("c a s -> c (a s)"),
                            w1k_r[:, 0, cols], w1k_r[:, 1, cols]).then_inc(ring_filled[bank], 1)
                    if name in ("P.v0", "P.v1", "P.v2", "P.v3"):
                        n = int(name[-1])
                        if n == 0:
                            drained(pe, ring_drained, st, "A.xT", 0, own=bank)
                        mm3(r, ctxU[:, :, :].rearrange("c a s -> c (a s)"), ctxL[:, :, :].rearrange("c a s -> c (a s)"),
                            wvo_r[:, 0, n, :], wvo_r[:, 1, n, :]).then_inc(ring_filled[bank], 1)
                    if name == "K.kT":
                        pe.wait_ge(k_kr, b.same(2, 2))
                        rows = slice(S * p, S * p + S)
                        mm(r[:, 0:S], ka[rows, 0, 0:128], ident[rows, rows], start=True, stop=True)
                        for k in range(1, PAIRS):
                            last = tr(r[:, S * k:S * k + S], ka[rows, k // 4, 128 * (k % 4):128 * (k % 4) + 128], ident[rows, rows])
                        last.then_inc(ring_filled[bank], 1)

                    if name in ("B.s0", "B.s1", "B.s2", "B.s3"):
                        g = int(name[-1])
                        if g == 0 and j == 0:
                            pe.wait_ge(a_st[p], b.same(7 * 16, 7 * 16))
                        mm(r, ident4[:, 0, :], window[:, j, :, :].rearrange("t h r -> t (h r)"), start=True, stop=False)
                        for k in range(4):
                            h = 4 * g + k
                            last = mm(r[:, 128 * k:128 * k + 128], qst[p][0:KS, h, j, :, :].rearrange("r e t -> r (e t)"),
                                      kst[p][0:KS, h, 128 * j:128 * j + 128], start=False, stop=k == 3)
                        last.then_inc(ring_filled[bank], 1)
                    if name in ("B.lin0", "B.lin1"):
                        i = int(name[-1])
                        if i == 0 and j == 0:
                            pe.wait_ge(a_st[p], b.same(7 * 16, 7 * 16))
                        for k in range(4):
                            for e in range(2):
                                h = 2 * (4 * i + k) + e
                                last = mm(r[64 * e:64 * e + 64, 128 * k:128 * k + 128], kst[p][0:KS, h, T:T + S],
                                          qst[p][0:KS, h, j, :, :].rearrange("r e t -> r (e t)"), start=True, stop=True)
                        last.then_inc(ring_filled[bank], 1)
                    if name in ("B.t0", "B.t1", "B.t2", "B.t3"):
                        g = int(name[-1])
                        pe.wait_ge(b_exp, b.tile(4, j, g + 1))
                        for k in range(4):
                            last = tr(r[:, 128 * k:128 * k + 128], pw[:, 4 * g + k, :], ident[:, :])
                        last.then_inc(ring_filled[bank], 1)
                    if name in ("B.pv0", "B.pv1", "B.pv2", "B.pv3"):
                        g = int(name[-1])
                        if g == 0:
                            wait(pe, b_comb, b.tile(3, j, 0))
                        drained(pe, ring_drained, st, f"B.t{g}", j)
                        for k in range(4):
                            h = 4 * g + k
                            last = mm(po[:, NVO * h:NVO * h + NVO], pt[:, h, :], vw[p][:, j, h, :, :].rearrange("r e d -> r (e d)"),
                                      start=True, stop=True)
                        last.then_inc(b_pv, 1)
                    if name == "B.lpv":
                        drained(pe, ring_drained, st, "B.lin1", j)
                        for k in range(PAIRS):
                            c = NVO * (H0 + k)
                            last = mm(po[:, c:c + NVO], wt[:, k, :], vbd[p][:, k, :], start=True, stop=True)
                        last.then_inc(b_pv, 1)
                    if name == "B.cT":
                        pe.wait_ge(b_comb, b.tile(3, j, 3))
                        for k in range(2):
                            last = tr(r[:, 128 * k:128 * k + 128], comb[:, k, :], ident[:, :])
                        last.then_inc(ring_filled[bank], 1)
                    if name == "B.op":
                        drained(pe, ring_drained, st, "B.cT", j, own=bank)
                        for k in range(2):
                            last = mm(r[:, 0:128], combT[:, k, :], wout_s[:, k, :], start=k == 0, stop=k == 1)
                        last.then_inc(ring_filled[bank], 1)
                    if name == "B.xT":
                        drained(pe, ring_drained, st, "B.op", j, own=bank)
                        tr(r[:, 0:128], x1[p][:, j, :], ident[:, :]).then_inc(ring_filled[bank], 1)

                    if name in ("C.q0", "C.q1"):
                        i = int(name[-1])
                        drained(pe, ring_drained, st.last, "B.xT", j, own=bank)
                        cols = slice(512 * i, 512 * i + 512)
                        mm3(r, x1U[p][:, j, :], x1L[p][:, j, :], w1q_r[:, 0, cols], w1q_r[:, 1, cols]).then_inc(ring_filled[bank], 1)
                    if name in ("C.t0", "C.t1"):
                        i = int(name[-1])
                        pe.wait_ge(c_qr, b.tile(2, j, i + 1))
                        for k in range(4):
                            last = tr(r[:, 128 * k:128 * k + 128], qa[:, i, 128 * k:128 * k + 128], ident[:, :])
                        last.then_inc(ring_filled[bank], 1)
                    if name in ("C.s0", "C.s1"):
                        i = int(name[-1])
                        if i == 0 and j == 0:
                            pe.wait_ge(k_mrow, b.at(1, 1))
                        drained(pe, ring_drained, st, f"C.t{i}", j, own=bank)
                        masked = mrow[p][:, :].rearrange("k (a s) -> k a s", a=1).broadcast_to([3, 8, S])
                        mm(r, ones3[:, :], masked, start=True, stop=False)
                        for k in range(4):
                            last = mm(r[:, 128 * k:128 * k + 128], qT[:, i, k, :], kbd[p][:, 4 * i + k, :],
                                      start=False, stop=k == 3)
                        last.then_inc(ring_filled[bank], 1)
                    if name in ("C.p0", "C.p1"):
                        i = int(name[-1])
                        pe.wait_ge(c_pn, b.tile(2, j, i + 1))
                        for k in range(4):
                            last = tr(r[:, 128 * k:128 * k + 128], pex[:, i, 128 * k:128 * k + 128], ident[:, :])
                        last.then_inc(ring_filled[bank], 1)
                    if name == "C.y":
                        if j == 0:
                            pe.wait_ge(k_vo[p], b.same(32, 32))
                        drained(pe, ring_drained, st, "C.p1", j, own=bank)
                        for k in range(PAIRS):
                            last = mm(r[:, 0:128], pT[:, k // 4, k % 4, :], vo[p][:, k, :], start=k == 0, stop=k == PAIRS - 1)
                        last.then_inc(ring_filled[bank], 1)

            run_steps(pe, emit, {1: prepare_values})

        @block.scalar
        def _(act):
            cp = nc.scalar.copy
            act.wait_ge(prep_pe, 1)
            cp(wkT[:, :], ring[:, 1, 0:128]).then_inc(prep_ev, 1)
            act.wait_ge(prep_pe, 2)
            cp(wkf_s[:, :], ring[:, 0, 0:128]).then_inc(prep_ev, 1)
            act.wait_ge(consts, 2)
            act.wait_ge(cleared, 12)

            def prepare_values(filled):
                for i in range(2):
                    act.wait_ge(prep_pe, 3 + i)
                    cp(pex[:, i, :], ring[:, 2 + i, :]).then_inc(prep_ev, 1)
                for n in range(4):
                    act.wait_ge(prep_pe, 5 + n)
                    cp(wvo_r[:, 0, n, :].bitcast(F32R), ring[:, 2 + n, :]).then_inc(prep_ev, 1)

            def emit(st):
                for name, j in ORDER:
                    b = stage_of(st, name)
                    if b is None:
                        continue
                    p = b.p
                    if (name, j) in RING:
                        bank, fill = st.ring(name, j)
                        r = ring[:, bank, :]

                    if name == "L.norm":
                        act.wait_ge(in_a[p], b.same(32, 32))
                        wait(act, a_ms, b.at(1, 0))
                        for k in range(NJ):
                            wait(act, a_ssq, b.at(2, k))
                            nc.scalar.activation(junk[:, :], xa[p][:, k, :], ACT.Square, accum_out=ssq[:, k:k + 1])\
                                .then_inc(a_ssq, 1)
                    if name == "A.qk":
                        act.wait_ge(ring_filled[bank], fill)
                        wait(act, a_out[1 - p], b.before(12 * 16))
                        wait(act, b_pv, b.at(5 * NJ, 5 * NJ) - 10 * NJ)
                        cp(hi[:, QK], r).then_inc(a_hi, 1)
                    if name == "A.mid":
                        drained(act, ring_drained, st, "A.qk", 0)
                        cp(mid[:, QK], rest[:, :]).then_inc(a_mid, 1)
                    if name == "A.vw":
                        act.wait_ge(ring_filled[bank], fill)
                        for k in range(NJ):
                            last = cp(vw[p][:, k, :, :, 0:HD0].rearrange("r h e d -> r e h d"),
                                      r[:, 256 * k:256 * k + 256].rearrange("r (e h d) -> r e h d", e=2, d=HD0))
                        last.then_inc(ring_drained[bank], 1)
                    if name == "A.enc":
                        act.wait_ge(ring_filled[bank], fill)
                        cp(hi[:, EN], r[:, 0:S]).then_inc(a_ehi, 1)
                    if name == "A.emid":
                        act.wait_ge(a_erest, b.at(1, 1))
                        cp(mid[:, EN], erest[:, :]).then_inc(a_emid, 1)
                    if name == "K.kT":
                        act.wait_ge(ring_filled[bank], fill)
                        for e in range(2):
                            q = slice(64 * e, 64 * e + 64)
                            last = cp(kbd[p][q, :, q], r[q, :].rearrange("d (k s) -> d k s", s=S))
                        last.then_inc(ring_drained[bank], 1)
                    if name in ("P.v0", "P.v1", "P.v2", "P.v3"):
                        n = int(name[-1])
                        e, i = n // 2, n % 2
                        act.wait_ge(ring_filled[bank], fill)
                        for q in range(2):
                            wait(act, k_vo[q], b.same(32, 0))
                        last = cp(vpair[:, e, 4 * i:4 * i + 4, :].rearrange("s k n -> s (k n)"), r)
                        last.then_inc(ring_drained[bank], 1)

                    if name in ("B.lin0", "B.lin1"):
                        i = int(name[-1])
                        act.wait_ge(ring_filled[bank], fill)
                        wait(act, b_pv, b.tile(5, j, 0))
                        last = nc.scalar.activation(wt[:, 4 * i:4 * i + 4, :].rearrange("s k t -> s (k t)"), r, ACT.Square,
                                                    bias=ones_col[:, :], scale=0.5)
                        last.then_inc(ring_drained[bank], 1)
                    if name in ("B.e0", "B.e1", "B.e2", "B.e3"):
                        g = int(name[-1])
                        drained(act, ring_drained, st, f"B.s{g}", j)
                        nc.scalar.activation(pw[:, 4 * g:4 * g + 4, :], pw[:, 4 * g:4 * g + 4, :], ACT.Exp,
                                             scale=float(HD0) ** -0.5).then_inc(b_exp, 1)
                    if name in ("B.t0", "B.t1", "B.t2", "B.t3"):
                        g = int(name[-1])
                        act.wait_ge(ring_filled[bank], fill)
                        last = cp(pt[:, 4 * g:4 * g + 4, :].rearrange("r h t -> r (h t)"), r)
                        last.then_inc(ring_drained[bank], 1)
                    if name == "B.cT":
                        act.wait_ge(ring_filled[bank], fill)
                        last = cp(combT[:, :, :].rearrange("c k t -> c (k t)"), r[:, 0:256])
                        last.then_inc(ring_drained[bank], 1)

                    if name in ("C.t0", "C.t1"):
                        i = int(name[-1])
                        act.wait_ge(ring_filled[bank], fill)
                        cp(qT[:, i, :, :].rearrange("d k t -> d (k t)"), r).then_inc(ring_drained[bank], 1)
                    if name in ("C.e0", "C.e1"):
                        i = int(name[-1])
                        drained(act, ring_drained, st, f"C.s{i}", j)
                        nc.scalar.activation(pex[:, i, :], pex[:, i, :], ACT.Exp, scale=HD1 ** -0.5).then_inc(c_exp, 1)
                    if name in ("C.p0", "C.p1"):
                        i = int(name[-1])
                        act.wait_ge(ring_filled[bank], fill)
                        cp(pT[:, i, :, :].rearrange("s k t -> s (k t)"), r).then_inc(ring_drained[bank], 1)

            run_steps(act, emit, {1: prepare_values})

        @block.vector
        def _(dve):
            v = nc.vector
            def upper(dst, src):
                return v.tensor_copy(dst.bitcast(F32R), src)

            v.memset(minus_half[:, :], -0.5).then_inc(consts, 1)
            v.memset(ones_col[:, :], 1.0).then_inc(consts, 1)
            v.memset(qst[0][:, :, :, :, :], 0.0).then_inc(stacks_cleared, 1)
            v.memset(kst[0][:, :, :], 0.0).then_inc(stacks_cleared, 1)
            v.memset(ones3[:, :], 1.0).then_inc(consts, 1)
            dve.wait_ge(loaded[0], n_loaded[0])
            v.tensor_copy(qfT[:, 1:H0, :], qfT[:, 0:1, :].broadcast_to([FD, H0 - 1, HD0])).then_inc(consts, 1)
            v.tensor_copy(kfT[:, 1:H0, :], kfT[:, 0:1, :].broadcast_to([FD, H0 - 1, HD0])).then_inc(consts, 1)
            for k in range(4):
                last = v.tensor_copy(ident4[:, k, :], ident[:, :])
            last.then_inc(consts, 1)
            upper(wq_r[:, 0, :], wq_s[:, :]).then_inc(w_upper, 1)
            upper(wwin_r[:, 0, :], wwin_s[:, 0:D]).then_inc(w_upper, 1)
            dve.wait_ge(prep_pe, 1)
            v.tensor_tensor(out=bd[:, :], in0=ring[:, 0, 0:128], in1=blocks[:, :], op=ALU.mult).then_inc(prep_ev, 1)
            for k in range(4):
                last = v.tensor_copy(window[:, :, k, :], window_f[:, :, :])
            last.then_inc(consts, 1)
            dve.wait_ge(cleared, 12)

            def rope(dst_a, dst_b, src, cos, sin, n, done):
                heads_n = src.shape[-1] // HD1
                v.tensor_tensor(out=dst_a.rearrange("t (h d) -> t h d", d=HD1), in0=src.rearrange("t (h d) -> t h d", d=HD1),
                                in1=cos.broadcast_to([n, heads_n, HD1]), op=ALU.mult)
                s4 = src.rearrange("t (h i two) -> t h i two", two=2, i=HD1 // 2)
                d4 = dst_b.rearrange("t (h i two) -> t h i two", two=2, i=HD1 // 2)
                c4 = sin.rearrange("t a (i two) -> t a i two", two=2)
                for e in range(2):
                    last = v.tensor_tensor(out=d4[:, :, :, e], in0=s4[:, :, :, 1 - e],
                                           in1=c4[:, :, :, e].broadcast_to([n, heads_n, HD1 // 2]), op=ALU.mult)
                last.then_inc(done, 1)

            def emit(st):
                for name, j in ORDER:
                    b = stage_of(st, name)
                    if b is None:
                        continue
                    p = b.p
                    if (name, j) in RING:
                        bank, fill = st.ring(name, j)
                        r = ring[:, bank, :]

                    if name == "L.norm":
                        dve.wait_ge(a_ssq, b.at(2, 2))
                        v.tensor_scalar(ms[:, :], ssq[:, :], 1.0 / D, 1e-6, ALU.mult, ALU.add).then_inc(a_ms, 1)
                        dve.wait_ge(a_rstd, b.at(1, 1))
                        for k in range(NJ):
                            v.tensor_scalar(xs[:, k, :], xa[p][:, k, :], rstd0[:, k:k + 1], None, ALU.mult).then_inc(a_xs, 1)
                    if name == "A.xT":
                        dve.wait_ge(ring_filled[bank], fill)
                        v.tensor_scalar(xnT[p][:, W:W + T], r[:, 0:T], nw_s[:, :], None, ALU.mult).then_inc(a_xnU, 1)
                        upper(ctxU[:, p, :], r[:, T:T + S]).then_inc(a_ctxU, 1)
                        dve.wait_ge(a_xnU, b.at(2, 1))
                        upper(xnU[:, :], xnT[p][:, W:W + T]).then_inc(a_xnU, 1)
                        dve.wait_ge(a_ctxU, b.at(1, 1))
                        v.tensor_tensor(out=ctxL[:, p, :].bitcast(F32R), in0=r[:, T:T + S], in1=ctxU[:, p, :], op=ALU.subtract)
                        dve.wait_ge(a_xnU, b.at(2, 2))
                        v.tensor_tensor(out=xnL[:, :].bitcast(F32R), in0=xnT[p][:, W:W + T], in1=xnU[:, :], op=ALU.subtract).then_inc(a_xnT, 1)
                        last = v.tensor_copy(ctxT[p][:, :, :], r[:, T:T + S].rearrange("c (a s) -> c a s", a=1).broadcast_to([D, 2, S]))
                        last.then_inc(ring_drained[bank], 1)
                    if name == "A.rest":
                        bank, fill = st.ring("A.qk", j)
                        dve.wait_ge(a_hi, b.at(1, 1))
                        wait(dve, a_lo, b.at(1, 0))
                        last = v.tensor_tensor(out=rest[:, :], in0=ring[:, bank, :], in1=hi[:, QK], op=ALU.subtract)
                        last.then_inc(ring_drained[bank], 1)
                    if name == "A.lo":
                        dve.wait_ge(a_mid, b.at(1, 1))
                        v.tensor_tensor(out=lo[:, QK], in0=rest[:, :], in1=mid[:, QK], op=ALU.subtract).then_inc(a_lo, 1)
                    if name == "A.enc":
                        dve.wait_ge(a_ehi, b.at(1, 1))
                        wait(dve, a_elo, b.at(1, 0))
                        v.tensor_tensor(out=erest[:, :], in0=r[:, 0:S], in1=hi[:, EN], op=ALU.subtract).then_inc(a_erest, 1)
                        for e in range(2):
                            q = slice(64 * e, 64 * e + 64)
                            src = r[q, S:S + D].rearrange("s (k e d) -> s k e d", e=2, d=HD0)
                            last = v.tensor_copy(vbd[p][q, :, 9 * e:9 * e + HD0], src[:, :, e, :])
                        last.then_inc(ring_drained[bank], 1)
                    if name == "A.elo":
                        dve.wait_ge(a_emid, b.at(1, 1))
                        v.tensor_tensor(out=lo[:, EN], in0=erest[:, :], in1=mid[:, EN], op=ALU.subtract).then_inc(a_elo, 1)

                    if name in ("P.k0", "P.k1"):
                        i = int(name[-1])
                        if i == 0:
                            for q in range(2):
                                dve.wait_ge(in_m[q], b.same(32, 32))
                            dve.wait_ge(loaded[2], n_loaded[2])
                            v.tensor_scalar(coskm[:, :], cosk[:, :], mcol[:, :], None, ALU.mult).then_inc(k_cos, 1)
                            v.tensor_scalar(sinkm[:, :], sink[:, :], mcol[:, :], None, ALU.mult).then_inc(k_cos, 1)
                            dve.wait_ge(k_cos, b.same(2, 2))
                            wait(dve, k_kr, b.same(2, 0))
                        dve.wait_ge(ring_filled[bank], fill)
                        one = "s (a d) -> s a d"
                        rope(ka[:, i, :], kb[:, i, :], r, coskm[:, :].rearrange(one, a=1),
                             sinkm[:, :].rearrange(one, a=1), 128, ring_drained[bank])
                    if name == "K.kT":
                        dve.wait_ge(in_m[p], b.same(32, 32))
                        v.tensor_scalar(mrow[p][:, :], mrow_u[p][:, :], -1.0, big3[:, :], ALU.add, ALU.mult).then_inc(k_mrow, 1)

                    if name in ("B.s0", "B.s1", "B.s2", "B.s3"):
                        g = int(name[-1])
                        dve.wait_ge(ring_filled[bank], fill)
                        v.tensor_reduce(out=mx[:, 4 * g:4 * g + 4], in_=r.rearrange("t (h r) -> t h r", r=128),
                                        axis=AX.X, op=ALU.max).then_inc(b_max, 1)
                    if name in ("B.d0", "B.d1", "B.d2", "B.d3"):
                        g = int(name[-1])
                        bank, _ = st.ring(f"B.s{g}", j)
                        dve.wait_ge(b_max, b.tile(4, j, g + 1))
                        top = mx[:, 4 * g:4 * g + 4].rearrange("t (h a) -> t h a", a=1).broadcast_to([128, 4, 128])
                        last = v.tensor_tensor(out=pw[:, 4 * g:4 * g + 4, :], in0=ring[:, bank, :].rearrange("t (h r) -> t h r", r=128),
                                               in1=top, op=ALU.subtract)
                        last.then_inc(ring_drained[bank], 1)
                    if name == "B.norm":
                        dve.wait_ge(b_pv, b.tile(5, j, 5))
                        lin = po[:, NVO * H0:NVO * (H0 + PAIRS)].rearrange("t (h d) -> t h d", d=HD0 + 1)
                        win = po[:, 0:NVO * H0].rearrange("t (h d) -> t h d", d=NVO)
                        v.tensor_scalar(den[:, 0, :], lin[:, :, HD0], 1e-6, None, ALU.add)
                        for e in range(2):
                            q = slice(64 * e, 64 * e + 64)
                            last = v.tensor_copy(den[q, 1, :], win[q, :, 9 * e + HD0])
                        last.then_inc(b_den, 1)
                        dve.wait_ge(b_den, b.tile(2, j, 1))
                        v.reciprocal(rden[:, :, :], den[:, :, :]).then_inc(b_den, 1)
                        dve.wait_ge(b_den, b.tile(2, j, 2))
                        v.tensor_tensor(out=comb[:, 0, :].rearrange("t (h d) -> t h d", d=HD0), in0=lin[:, :, 0:HD0],
                                        in1=rden[:, 0, :].rearrange("t (h a) -> t h a", a=1).broadcast_to([128, H0, HD0]),
                                        op=ALU.mult).then_inc(b_comb, 1)
                        for e in range(2):
                            q = slice(64 * e, 64 * e + 64)
                            v.tensor_tensor(out=comb[q, 1, :].rearrange("t (h d) -> t h d", d=HD0),
                                            in0=win[q, :, 9 * e:9 * e + HD0],
                                            in1=rden[q, 1, :].rearrange("t (h a) -> t h a", a=1).broadcast_to([64, H0, HD0]),
                                            op=ALU.mult).then_inc(b_comb, 1)
                    if name == "B.op":
                        dve.wait_ge(ring_filled[bank], fill)
                        dve.wait_ge(in_r[p], b.same(16, 16))
                        last = v.tensor_tensor(out=x1[p][:, j, :], in0=r[:, 0:128], in1=xr[p][:, j, :], op=ALU.add)
                        last.then_inc(ring_drained[bank], 1)

                    if name == "B.xT":
                        dve.wait_ge(ring_filled[bank], fill)
                        upper(x1U[p][:, j, :], r[:, 0:128]).then_inc(b_x1U, 1)
                        dve.wait_ge(b_x1U, b.tile(1, j, 1))
                        v.tensor_tensor(out=x1L[p][:, j, :].bitcast(F32R), in0=r[:, 0:128], in1=x1U[p][:, j, :], op=ALU.subtract)\
                            .then_inc(ring_drained[bank], 1)

                    if name in ("C.q0", "C.q1"):
                        i = int(name[-1])
                        dve.wait_ge(ring_filled[bank], fill)
                        wait(dve, c_qr, b.tile(2, j, i + 1) - 2)
                        rope(qa[:, i, :], qb[:, i, :], r, cosq[:, j:j + 1, :], sinq[:, j:j + 1, :], 128, ring_drained[bank])
                    if name in ("C.s0", "C.s1"):
                        i = int(name[-1])
                        dve.wait_ge(ring_filled[bank], fill)
                        wait(dve, c_pn, b.tile(2, j, i + 1) - 2)
                        v.tensor_reduce(out=mx1[:, 8 * i:8 * i + 8], in_=r.rearrange("t (h s) -> t h s", s=S),
                                        axis=AX.X, op=ALU.max).then_inc(c_max, 1)
                    if name in ("C.d0", "C.d1"):
                        i = int(name[-1])
                        bank, _ = st.ring(f"C.s{i}", j)
                        dve.wait_ge(c_max, b.tile(2, j, i + 1))
                        top = mx1[:, 8 * i:8 * i + 8].rearrange("t (h a) -> t h a", a=1).broadcast_to([128, 8, S])
                        v.tensor_tensor(out=pex[:, i, :].rearrange("t (h s) -> t h s", s=S),
                                        in0=ring[:, bank, :].rearrange("t (h s) -> t h s", s=S), in1=top,
                                        op=ALU.subtract).then_inc(ring_drained[bank], 1)
                    if name in ("C.n0", "C.n1"):
                        i = int(name[-1])
                        q = slice(8 * i, 8 * i + 8)
                        dve.wait_ge(c_exp, b.tile(2, j, i + 1))
                        v.tensor_reduce(out=lsum[:, q], in_=pex[:, i, :].rearrange("t (h s) -> t h s", s=S), axis=AX.X,
                                        op=ALU.add).then_inc(c_sum, 1)
                        dve.wait_ge(c_sum, b.tile(2, j, i + 1))
                        v.reciprocal(rsum[:, q], lsum[:, q]).then_inc(c_rsum, 1)
                    if name == "C.y":
                        dve.wait_ge(ring_filled[bank], fill)
                        wait(dve, c_zn, b.tile(1, j, 0))
                        v.tensor_tensor(out=z[:, :], in0=r[:, 0:128], in1=x1[p][:, j, :], op=ALU.add)\
                            .then_inc(c_z, 1)
                        dve.wait_ge(c_z, b.tile(1, j, 1))
                        v.bn_stats(stats[:, :], z[:, :]).then_inc(ring_drained[bank], 1)
                        dve.wait_ge(loaded[0], n_loaded[0])
                        dve.wait_ge(ring_drained[bank], fill)
                        v.bn_aggr(mv[:, :], stats[:, :]).then_inc(c_var, 1)
                        dve.wait_ge(c_var, b.tile(1, j, 1))
                        v.tensor_scalar(veps[:, :], mv[:, 1:2], 1e-3, None, ALU.add).then_inc(c_veps, 1)
                    if name == "C.fin":
                        dve.wait_ge(c_rstd, b.tile(1, j, 1))
                        wait(dve, c_zg, b.tile(1, j, 0))
                        v.tensor_scalar(zn[:, :], z[:, :], mv[:, 0:1], rstd1[:, :], ALU.subtract, ALU.mult).then_inc(c_zn, 1)

            def split_values(filled):
                for n in range(4):
                    dve.wait_ge(prep_ev, 6 + n)
                    v.tensor_tensor(out=wvo_r[:, 1, n, :].bitcast(F32R), in0=ring[:, 2 + n, :], in1=wvo_r[:, 0, n, :],
                                    op=ALU.subtract).then_inc(w_rest, 1)
                dve.wait_ge(loaded[2], n_loaded[2])
                for part, src in ((w1k_r, qb), (w1q_r, qa)):
                    upper(part[:, 0, :], src[:, :, :].rearrange("c a n -> c (a n)")).then_inc(w_upper, 1)

            run_steps(dve, emit, {1: split_values})

        @block.gpsimd
        def _(pool):
            g = nc.gpsimd
            n = 0
            for p in range(2):
                for part, value in ((xnT[p][:, 0:W], 0.0), (vw[p][:, :, :, :, :], 1.0), (vbd[p][:, :, :], 0.0),
                                    (vbd[p][0:64, :, HD0:HD0 + 1], 1.0), (vbd[p][64:128, :, NVO - 1:NVO], 1.0),
                                    (kbd[p][:, :, :], 0.0)):
                    wait(pool, cleared, n)
                    g.memset(part, value).then_inc(cleared, 1)
                    n += 1
            pool.wait_ge(consts, 1)

            def emit(st):
                for name, j in ORDER:
                    b = stage_of(st, name)
                    if b is None:
                        continue
                    p = b.p
                    if name == "L.norm":
                        pool.wait_ge(a_ms, b.at(1, 1))
                        wait(pool, a_xs, b.at(2, 0))
                        g.tensor_tensor(out=rstd0[:, :], in0=ms[:, :], in1=minus_half[:, :], op=ALU.pow).then_inc(a_rstd, 1)
                    if name in ("P.k0", "P.k1"):
                        i = int(name[-1])
                        drained(pool, ring_drained, st, name, j)
                        g.tensor_tensor(out=ka[:, i, :], in0=ka[:, i, :], in1=kb[:, i, :], op=ALU.add).then_inc(k_kr, 1)
                    if name in ("C.q0", "C.q1"):
                        i = int(name[-1])
                        drained(pool, ring_drained, st, name, j)
                        g.tensor_tensor(out=qa[:, i, :], in0=qa[:, i, :], in1=qb[:, i, :], op=ALU.add).then_inc(c_qr, 1)
                    if name in ("C.n0", "C.n1"):
                        i = int(name[-1])
                        pool.wait_ge(c_rsum, b.tile(2, j, i + 1))
                        rs = rsum[:, 8 * i:8 * i + 8].rearrange("t (h a) -> t h a", a=1).broadcast_to([128, 8, S])
                        g.tensor_tensor(out=pex[:, i, :].rearrange("t (h s) -> t h s", s=S),
                                        in0=pex[:, i, :].rearrange("t (h s) -> t h s", s=S), in1=rs, op=ALU.mult)\
                            .then_inc(c_pn, 1)
                    if name == "C.y":
                        pool.wait_ge(c_veps, b.tile(1, j, 1))
                        g.tensor_tensor(out=rstd1[:, :], in0=veps[:, :], in1=minus_half[:, 0:1], op=ALU.pow).then_inc(c_rstd, 1)
                    if name == "C.fin":
                        pool.wait_ge(c_zn, b.tile(1, j, 1))
                        g.tensor_tensor(out=zg[:, :], in0=zn[:, :], in1=gamma_s[:, :], op=ALU.mult).then_inc(c_zg, 1)
                        pool.wait_ge(c_zg, b.tile(1, j, 1))
                        wait(pool, c_out[j], b.at(16, 0))
                        g.tensor_tensor(out=yo[:, j, :], in0=zg[:, :], in1=beta_s[:, :], op=ALU.add).then_inc(c_yo, 1)

            def rest(n, weights, parts):
                pool.wait_ge(w_upper, n)
                g.tensor_tensor(out=parts[:, 1, :].bitcast(F32R), in0=weights, in1=parts[:, 0, :], op=ALU.subtract)\
                    .then_inc(w_rest, 1)

            rest(1, wq_s[:, :], wq_r)
            rest(2, wwin_s[:, 0:D], wwin_r)

            def rest_later(filled):
                rest(3, qb[:, :, :].rearrange("c a n -> c (a n)"), w1k_r)
                rest(4, qa[:, :, :].rearrange("c a n -> c (a n)"), w1q_r)

            def clear_odd(filled):
                g.memset(qst[1][:, :, :, :, :], 0.0).then_inc(stacks_cleared, 1)
                g.memset(kst[1][:, :, :], 0.0).then_inc(stacks_cleared, 1)

            def wait_loads(filled):
                pool.wait_ge(loaded[2], n_loaded[2])

            run_steps(pool, emit, {0: clear_odd, 1: rest_later, 2: wait_loads})


def constants():
    f = np.float32
    t = np.arange(128)
    r = np.arange(128)
    tt, rr = (t % W)[:, None], r[None, :]
    ok = (rr >= tt) & (rr <= tt + W)
    first = ok & ((rr >= W) | (t[:, None] >= W))
    window = np.where(np.stack([first, ok], 1), f(0), f(-1e30)).astype(f)
    blk = np.arange(128) // HD0
    blocks = (blk[:, None] == blk[None, :]).astype(f)
    inv = (f(1.0) / np.power(f(10000.0), np.arange(0, HD1, 2, dtype=f) / f(HD1))).astype(f)
    ang = (np.arange(T, dtype=f)[:, None] * inv[None, :]).astype(f)
    cos, sin = np.cos(ang).astype(f), np.sin(ang).astype(f)
    rope = np.stack([np.repeat(cos, 2, 1), np.stack([-sin, sin], -1).reshape(T, HD1)]).astype(f)
    left, big = f(BIG), []
    for _ in range(3):
        top = (left.view(np.uint32) & np.uint32(0xFFFF0000)).view(f)
        big.append(top)
        left = f(left - top)
    return {"tab_ident": np.eye(128, dtype=f), "tab_window": window, "tab_blocks": blocks, "tab_rope": rope,
            "tab_big": np.array(big, f).reshape(3, 1)}


_INS = ["x", "ctx_1024", "mask_BxS2_bf1", "L0_xattn_norm_w", "L0_xattn_Wq", "L0_xattn_Wkv", "L0_xattn_Wqf",
        "L0_xattn_Wkf", "L0_xattn_Wwin", "L0_xattn_Wout", "L1_xattn_Wq", "L1_xattn_Wk", "L1_xattn_Wv", "L1_xattn_Wo",
        "L1_xattn_ln_gamma", "L1_xattn_ln_beta"]


def kernel(**inputs):
    import concourse.bacc as bacc
    from concourse.bass_utils import run_bass_kernel_spmd

    nc = bacc.Bacc("TRN2", target_bir_lowering=False, num_devices=1)
    arrays, args = {}, []
    for name in _INS:
        a = np.ascontiguousarray(inputs[name])
        if a.dtype == np.bool_:
            a = a.view(np.uint8)
        if name in ("L0_xattn_Wqf", "L0_xattn_Wkf"):
            a = np.ascontiguousarray(a.T)
        arrays["in_" + name] = a
        args.append(nc.dram_tensor("in_" + name, a.shape, mybir.dt.from_np(a.dtype), kind="ExternalInput").ap())
    for name, a in constants().items():
        arrays[name] = a
        args.append(nc.dram_tensor(name, a.shape, F32, kind="ExternalInput").ap())
    out = nc.dram_tensor("out_0", (NB, T, D), F32, kind="ExternalOutput").ap()
    scratch = [[nc.dram_tensor(f"stack{p}_{n}", (SLOTS, HD0, H0, T + n * S), BF16, kind="Internal").ap() for n in range(2)]
               for p in range(2)]
    build(nc, *args, out, scratch)
    r = run_bass_kernel_spmd(nc, [arrays], core_ids=[0])
    return r.results[0]["out_0"]
```
